# Optimizing a Trainium2 kernel written in Bass

```python
import numpy as np
import jax
import jax.numpy as jnp

def _softmax(x, axis=-1):
    return jax.nn.softmax(x, axis=axis)

def _gelu(x):
    return jax.nn.gelu(x, approximate=True)

def _silu(x):
    return jax.nn.silu(x)

def _sigmoid(x):
    return jax.nn.sigmoid(x)

def _layernorm(x, axis=-1, eps=1e-05):
    m = jnp.mean(x, axis=axis, keepdims=True)
    v = jnp.var(x, axis=axis, keepdims=True)
    return (x - m) / jnp.sqrt(v + eps)

def _scatter_add(tgt, idx, src, axis=0):
    return tgt.at[idx].add(src)

def _segment_sum(src, seg, n):
    return jax.ops.segment_sum(src, seg, n)
kernel_name = 'mk_metaformer_d1_conv_nchw256_r4_f9a9d7'

def setup_inputs(seed: int=0):
    np.random.seed(seed)
    _w = jnp.asarray

    def _rec_inputs():
        import jax
        import jax.numpy as jnp
        _gk = jax.random.key(seed)
        x = -0.000125 + 0.9999 * jax.random.normal(jax.random.fold_in(_gk, 1), (8, 64, 32, 32), jnp.float32)
        return x
    x = _rec_inputs()

    def _L0_conv_setup():
        import math
        import jax, jax.numpy as jnp
        import numpy as np
        B, C_IN, C_MID, H, W = (8, 64, 16, 32, 32)
        N_ANGLES = 8
        RADIUS_WIDTH = 8
        OVERLAP_RATIO = 1.5
        EPS = 1e-08

        def _build_masks(H, W):
            cy, cx = (H // 2, W // 2)
            y = jnp.arange(H, dtype=jnp.float32)[:, None] - cy
            x = jnp.arange(W, dtype=jnp.float32)[None, :] - cx
            r = jnp.sqrt(y * y + x * x)
            theta = (jnp.arctan2(y, x) + math.pi) % math.pi
            max_r = max(cy, cx)
            n_radii = int(max_r // RADIUS_WIDTH) + 1
            radius_idx = jnp.clip(jnp.floor(r / RADIUS_WIDTH).astype(jnp.int32), 0, n_radii - 1)
            delta = math.pi / N_ANGLES
            half_width = OVERLAP_RATIO * delta / 2.0
            centers = (jnp.arange(N_ANGLES, dtype=jnp.float32) * delta + delta / 2.0)[:, None, None]
            dist = jnp.abs(theta[None] - centers)
            w = jnp.clip(1.0 - dist / half_width, 0.0) * (dist < half_width)
            angle_weights = w / (w.sum(axis=0, keepdims=True) + EPS)
            return (radius_idx, angle_weights, n_radii)

        def _forward(x, w_in, w_out, bin_weights):
            Hh, Ww = x.shape[-2:]
            radius_idx, angle_weights, _ = _build_masks(Hh, Ww)
            x_proj = jnp.einsum('bchw,mc->bmhw', x, w_in)
            x_fft = jnp.fft.fftshift(jnp.fft.fft2(x_proj, norm='ortho'), axes=(-2, -1))
            mag = jnp.abs(x_fft) + EPS
            wt = bin_weights[:, :, radius_idx]
            gain = jnp.einsum('ahw,cahw->chw', angle_weights, wt)
            phase = jnp.angle(x_fft)
            enh = mag * gain[None] * (jnp.cos(phase) + 1j * jnp.sin(phase))
            x_enh = jnp.fft.ifft2(jnp.fft.ifftshift(enh, axes=(-2, -1)), norm='ortho').real
            x_enh = jnp.einsum('bmhw,cm->bchw', x_enh, w_out)
            return x + x_enh
        key = jax.random.key(seed)
        k1, k2, k3, k4 = jax.random.split(key, 4)
        _, _, n_radii = _build_masks(H, W)
        x = jax.random.normal(k1, (B, C_IN, H, W), dtype=jnp.float32)
        w_in = jax.random.normal(k2, (C_MID, C_IN), dtype=jnp.float32) * math.sqrt(2.0 / C_MID)
        w_out = jax.random.normal(k3, (C_IN, C_MID), dtype=jnp.float32) * math.sqrt(2.0 / C_IN)
        bin_weights = 1.0 + 0.1 * jax.random.normal(k4, (C_MID, N_ANGLES, n_radii), dtype=jnp.float32)
        return {'x': x, 'w_in': w_in, 'w_out': w_out, 'bin_weights': bin_weights}
    _L0_conv_all = _L0_conv_setup()
    _L0_conv_in = {k: v for k, v in _L0_conv_all.items() if k in ('w_in', 'w_out', 'bin_weights')}
    del _L0_conv_all

    def _L0_ffn_setup():
        import jax, jax.numpy as jnp
        import numpy as np
        D_MODEL = 64
        N_EXPERTS = 16
        HIDDEN = 128
        SCALE = 0.02
        key = jax.random.key(seed)
        ks = jax.random.split(key, 5)
        x = jax.random.normal(ks[0], (4, 2048, D_MODEL), dtype=jnp.float32)
        gate_w = jax.random.normal(ks[1], (D_MODEL, N_EXPERTS), dtype=jnp.float32) * SCALE
        gate_b = jnp.zeros((N_EXPERTS,), dtype=jnp.float32)
        w1 = jax.random.normal(ks[2], (N_EXPERTS, D_MODEL, HIDDEN), dtype=jnp.float32) * SCALE
        w2 = jax.random.normal(ks[3], (N_EXPERTS, D_MODEL, HIDDEN), dtype=jnp.float32) * SCALE
        w3 = jax.random.normal(ks[4], (N_EXPERTS, HIDDEN, D_MODEL), dtype=jnp.float32) * SCALE
        return {'x': x, 'gate_w': gate_w, 'gate_b': gate_b, 'w1': w1, 'w2': w2, 'w3': w3}
    _L0_ffn_all = _L0_ffn_setup()
    _L0_ffn_in = {k: v for k, v in _L0_ffn_all.items() if k in ('gate_w', 'gate_b', 'w1', 'w2', 'w3')}
    del _L0_ffn_all
    return {'x': x, 'L0_conv_w_in': _L0_conv_in['w_in'], 'L0_conv_w_out': _L0_conv_in['w_out'], 'L0_conv_bin_weights': _L0_conv_in['bin_weights'], 'L0_ffn_gate_w': _L0_ffn_in['gate_w'], 'L0_ffn_gate_b': _L0_ffn_in['gate_b'], 'L0_ffn_w1': _L0_ffn_in['w1'], 'L0_ffn_w2': _L0_ffn_in['w2'], 'L0_ffn_w3': _L0_ffn_in['w3']}

def reference(x, L0_conv_w_in, L0_conv_w_out, L0_conv_bin_weights, L0_ffn_gate_w, L0_ffn_gate_b, L0_ffn_w1, L0_ffn_w2, L0_ffn_w3):
    import jax
    import jax.numpy as jnp

    def _L0_conv_ref(x, w_in, w_out, bin_weights):
        import math
        import jax, jax.numpy as jnp
        import numpy as np
        B, C_IN, C_MID, H, W = (8, 64, 16, 32, 32)
        N_ANGLES = 8
        RADIUS_WIDTH = 8
        OVERLAP_RATIO = 1.5
        EPS = 1e-08

        def _build_masks(H, W):
            cy, cx = (H // 2, W // 2)
            y = jnp.arange(H, dtype=jnp.float32)[:, None] - cy
            x = jnp.arange(W, dtype=jnp.float32)[None, :] - cx
            r = jnp.sqrt(y * y + x * x)
            theta = (jnp.arctan2(y, x) + math.pi) % math.pi
            max_r = max(cy, cx)
            n_radii = int(max_r // RADIUS_WIDTH) + 1
            radius_idx = jnp.clip(jnp.floor(r / RADIUS_WIDTH).astype(jnp.int32), 0, n_radii - 1)
            delta = math.pi / N_ANGLES
            half_width = OVERLAP_RATIO * delta / 2.0
            centers = (jnp.arange(N_ANGLES, dtype=jnp.float32) * delta + delta / 2.0)[:, None, None]
            dist = jnp.abs(theta[None] - centers)
            w = jnp.clip(1.0 - dist / half_width, 0.0) * (dist < half_width)
            angle_weights = w / (w.sum(axis=0, keepdims=True) + EPS)
            return (radius_idx, angle_weights, n_radii)

        def _forward(x, w_in, w_out, bin_weights):
            Hh, Ww = x.shape[-2:]
            radius_idx, angle_weights, _ = _build_masks(Hh, Ww)
            x_proj = jnp.einsum('bchw,mc->bmhw', x, w_in)
            x_fft = jnp.fft.fftshift(jnp.fft.fft2(x_proj, norm='ortho'), axes=(-2, -1))
            mag = jnp.abs(x_fft) + EPS
            wt = bin_weights[:, :, radius_idx]
            gain = jnp.einsum('ahw,cahw->chw', angle_weights, wt)
            phase = jnp.angle(x_fft)
            enh = mag * gain[None] * (jnp.cos(phase) + 1j * jnp.sin(phase))
            x_enh = jnp.fft.ifft2(jnp.fft.ifftshift(enh, axes=(-2, -1)), norm='ortho').real
            x_enh = jnp.einsum('bmhw,cm->bchw', x_enh, w_out)
            return x + x_enh
        return _forward(x, w_in, w_out, bin_weights)

    def _L0_ffn_ref(x, gate_w, gate_b, w1, w2, w3):
        import jax, jax.numpy as jnp
        import numpy as np
        D_MODEL = 64
        N_EXPERTS = 16
        HIDDEN = 128
        SCALE = 0.02
        n_experts = w1.shape[0]
        logits = jnp.einsum('bsd,de->bse', x, gate_w) + gate_b
        probs = jax.nn.softmax(logits, axis=-1)
        top_probs, top_idx = jax.lax.top_k(probs, 2)
        top_probs = top_probs / jnp.sum(top_probs, axis=-1, keepdims=True)
        dispatch = jnp.sum(jax.nn.one_hot(top_idx, n_experts, dtype=x.dtype) * top_probs[..., None], axis=-2)
        h1 = jnp.einsum('bsd,edh->bseh', x, w1)
        h2 = jnp.einsum('bsd,edh->bseh', x, w2)
        hidden = jax.nn.silu(h1) * h2
        expert_out = jnp.einsum('bseh,eho->bseo', hidden, w3)
        return jnp.einsum('bseo,bse->bso', expert_out, dispatch)

    def _gn(v, G=32, eps=1e-05):
        B_, C_, H_, W_ = v.shape
        g = v.reshape(B_, G, C_ // G, H_, W_)
        m = jnp.mean(g, axis=(2, 3, 4), keepdims=True)
        s = jnp.var(g, axis=(2, 3, 4), keepdims=True)
        return ((g - m) / jnp.sqrt(s + eps)).reshape(v.shape)

    def _ln_c(v, eps=1e-06):
        m = jnp.mean(v, axis=1, keepdims=True)
        s = jnp.var(v, axis=1, keepdims=True)
        return (v - m) / jnp.sqrt(s + eps)

    def _ln_t(v, eps=1e-05):
        m = jnp.mean(v, axis=-1, keepdims=True)
        s = jnp.var(v, axis=-1, keepdims=True)
        return (v - m) / jnp.sqrt(s + eps)

    def _to_tokens(v):
        B_, C_, H_, W_ = v.shape
        return v.reshape(B_, C_, H_ * W_).transpose(0, 2, 1)

    def _from_tokens(t, like):
        B_, C_, H_, W_ = like.shape
        return t.transpose(0, 2, 1).reshape(B_, C_, H_, W_)
    x = x + _L0_conv_ref(_ln_c(x), L0_conv_w_in, L0_conv_w_out, L0_conv_bin_weights)
    t = _to_tokens(x)
    t = t + _L0_ffn_ref(_ln_t(t), L0_ffn_gate_w, L0_ffn_gate_b, L0_ffn_w1, L0_ffn_w2, L0_ffn_w3)
    x = _from_tokens(t, x)
    return x

_drawn_inputs = setup_inputs


def setup_inputs(seed=0):
    import zlib

    import numpy as np

    out = dict(_drawn_inputs(seed))
    spreads = {'L0_ffn_gate_b': (0.0, 0.8)}
    factors = {'L0_ffn_gate_w': 8.0, 'L0_ffn_w1': 8.0, 'L0_ffn_w2': 8.0, 'L0_ffn_w3': 8.0}
    for name, (base, spread) in spreads.items():
        noise = np.random.default_rng([zlib.crc32(name.encode()), seed]).standard_normal(out[name].shape)
        drawn = base * np.exp(spread * noise) if base else spread * noise
        out[name] = jnp.asarray(drawn.astype(out[name].dtype))
    for name, factor in factors.items():
        out[name] = (out[name] * factor).astype(out[name].dtype)
    return out
```

```python
from contextlib import ExitStack

import numpy as np

import concourse.bass as bass
from concourse import mybir

F32 = mybir.dt.float32
F16 = mybir.dt.float16
ALU = mybir.AluOpType
ACT = mybir.ActivationFunctionType
AX_X = mybir.AxisListType.X

B, C, H, W = 8, 64, 32, 32
M = 16
N_ANGLES, RADIUS_WIDTH, OVERLAP = 8, 8, 1.5
N_RADII = max(H // 2, W // 2) // RADIUS_WIDTH + 1
AR = N_ANGLES * N_RADII
E, HID = 16, 128
P = 128
G = B // 2
PIX = H * W
COLS = G * PIX
BLK = 512
NBLK = COLS // BLK
QUADS, KT, QPIX = 4, 2, PIX // 4
CHUNKS = 16
TOK = COLS * 2 // CHUNKS
SUB = TOK // P
TILES = CHUNKS * SUB
EPS_CONV_LN, EPS_FFN_LN, EPS_MAG = 1e-6, 1e-5, 1e-8
SQRT_MIN = 2.0 ** -116
WSCALE = 64.0
FAR = 1e30
PAIRS = E // 2
FIN_AT = 4


def first_chunk(c):
    return isinstance(c, int) and c == 0


def last_chunk(c):
    return isinstance(c, int) and c == CHUNKS - 1


def wait_past(eng, semaphore, value):
    if not isinstance(value, int) or value > 0:
        eng.wait_ge(semaphore, value)


def over_chunks(eng, chunk):
    chunk(0, 0, 1)
    with eng.Fori(0, CHUNKS // 2 - 1) as i:
        chunk(2 * i + 1, 1, i + 1)
        chunk(2 * i + 2, 0, i + 2)
    chunk(CHUNKS - 1, 1, CHUNKS // 2)


def hartley_tables():
    xy = np.arange(QPIX)
    x, y = xy // 16, xy % 16
    out = []
    for sign in (1.0, -1.0):
        t = np.empty((QPIX, 4, QPIX))
        for cls in range(4):
            u, v = 2 * x + cls // 2, 2 * y + cls % 2
            th = 2 * np.pi * ((np.outer(x, u) + np.outer(y, v)) % 32) / 32
            t[:, cls] = (np.cos(th) + sign * np.sin(th)) / 32
        out.append(t)
    fwd, neg = out
    inv = fwd.transpose(2, 1, 0)
    tile = lambda t: np.ascontiguousarray(t.reshape(KT, P, 4, QPIX).transpose(1, 0, 2, 3).reshape(P, -1).astype(np.float32))
    return tile(fwd), tile(neg), tile(inv)


def bin_table():
    f = np.float32
    y = np.arange(H, dtype=f)[:, None] - f(H // 2)
    x = np.arange(W, dtype=f)[None, :] - f(W // 2)
    r = np.sqrt(y * y + x * x)
    theta = (np.arctan2(y, x) + f(np.pi)) % f(np.pi)
    ridx = np.clip(np.floor(r / f(RADIUS_WIDTH)).astype(np.int32), 0, N_RADII - 1)
    delta = np.pi / N_ANGLES
    half = OVERLAP * delta / 2.0
    centers = (np.arange(N_ANGLES, dtype=f) * f(delta) + f(delta / 2.0))[:, None, None]
    dist = np.abs(theta[None] - centers)
    w = np.clip(f(1.0) - dist / f(half), f(0.0), None) * (dist < f(half))
    w = w / (w.sum(axis=0, keepdims=True) + f(1e-8))
    full = w[:, None] * (ridx[None, None] == np.arange(N_RADII)[None, :, None, None])
    full = np.fft.ifftshift(full.astype(np.float64), axes=(-2, -1))
    flip = np.roll(full[:, :, ::-1, ::-1], 1, axis=(-2, -1))
    sym = (full + flip) / 2
    a = np.arange(QPIX)
    cols = [sym[:, :, 2 * (a // 16) + cls // 2, 2 * (a % 16) + cls % 2] for cls in range(4)]
    return np.ascontiguousarray(np.stack(cols, 2).reshape(AR, PIX).astype(f))


def constant_tile():
    eye = np.eye(P)
    mean = np.kron(np.eye(2), np.full((C, C), 1.0 / C))
    rev = np.broadcast_to(E - np.arange(E), (P, E))
    return np.ascontiguousarray(np.concatenate([eye, eye - mean, mean, rev], 1).astype(np.float32))


def build(nc, x, w_in, w_out, bin_w, gate_w, gate_b, w1, w2, w3, t_const, t_fwd, t_neg, t_inv, t_bins, out):
    ctx = ExitStack()
    with ctx:
        def sb(name, shape, dt=F32):
            return ctx.enter_context(nc.sbuf_tensor(name, shape, dt))

        def sem(name):
            return ctx.enter_context(nc.semaphore(name))

        cst = sb("cst", [P, 3 * P + E])
        ident, centre, mean64, rev_iota = cst[:, 0:P], cst[:, P:2 * P], cst[:, 2 * P:3 * P], cst[:, 3 * P:3 * P + E]
        ident16 = sb("ident16", [P, P], F16)
        eps_conv, eps_ffn = sb("eps_conv", [P, 1]), sb("eps_ffn", [P, 1])
        w_in_bd = sb("w_in_bd", [P, 2 * M])
        w_out_bd = sb("w_out_bd", [P, P])
        bw_rows = sb("bw_rows", [AR, M])
        bw_cols = sb("bw_cols", [AR, B, M])
        shared = sb("shared", [P, 8, PIX])
        fwd, neg, inv = (shared[:, 2 * n:2 * n + 2, :].rearrange("p k (c n) -> p k c n", c=4) for n in range(3))
        bins = shared[0:AR, 6, :]
        filt_t = shared[:, 7, :].rearrange("p (c k n) -> p c k n", c=4, k=KT)
        xab = shared[:, :, :].rearrange("p a n -> p (a n)").bitcast(F16).rearrange("p (c a n) -> p c a n", c=CHUNKS, a=2)
        gate_raw = sb("gate_raw", [P, E])
        gate_hi, gate_lo = sb("gate_hi", [P, E], F16), sb("gate_lo", [P, E], F16)
        gate_b_all = sb("gate_b_all", [P, E])
        w1_raw, w2_raw = sb("w1_raw", [P, E, HID]), sb("w2_raw", [P, E, HID])
        w1_hi, w2_hi = sb("w1_hi", [P, E, HID], F16), sb("w2_hi", [P, E, HID], F16)
        w12_lo = sb("w12_lo", [P, E, HID], F16)
        w3_sb = sb("w3_sb", [P, E, C])
        xs = sb("xs", [P, COLS])
        ln = sb("ln", [P, COLS])
        sq = sb("sq", [P, 2, BLK])
        std = sb("std", [P, 2, BLK])
        rstd = sb("rstd", [P, 2, BLK])
        half_b = sb("half_b", [P, BLK])
        fold1 = sb("fold1", [P, 2, 2, QPIX])
        fold2 = sb("fold2", [P, 4, QPIX])
        power = sb("power", [P, 2, 2, BLK])
        pw = sb("pw", [P, 2, BLK])
        pwc = sb("pwc", [P, 2, BLK])
        mag = sb("mag", [P, 2, BLK])
        rmag = sb("rmag", [P, 2, BLK])
        unit = sb("unit", [P, 2, BLK])
        unit1 = sb("unit1", [P, 2, BLK])
        zed = sb("zed", [P, 2, BLK])
        filt = sb("filt", [P, 4, QPIX])
        enh = sb("enh", [P, 4, QPIX])
        cen = ln[:, :].rearrange("p (t c) -> p t c", t=TILES)
        cen_sq = sb("cen_sq", [P, 2, 8 * C])
        ssq = sb("ssq", [P, TILES])
        std_t, rstd_t = sb("std_t", [P, TILES]), sb("rstd_t", [P, TILES])
        tok = sb("tok", [P, 2, SUB, C])
        parts = sb("parts", [P, 2, SUB, 3, C], F16)
        lg, lg2, cand, first, second = (t[:, :, :].rearrange("p k (t e) -> p (k t) e", e=E)
                                        for t in (mag, rmag, unit, unit1, zed))
        m1, m2, top = sb("m1", [P, TILES]), sb("m2", [P, TILES]), sb("top", [P, TILES])
        gap, ratio, wt1, wt2 = (sb(n, [P, TILES]) for n in ("gap", "ratio", "wt1", "wt2"))
        disp = sb("disp", [P, TILES, E])
        gated = sb("gated", [P, 2, TOK])
        hid = sb("hid", [P, 2, TOK])
        xc = sb("xc", [P, 2, 2, TOK], F16)
        prod = sb("prod", [P, 2, SUB, 2, C])
        acc = sb("acc", [P, SUB, 2, C])
        ffn = sb("ffn", [P, SUB, C])
        res = sb("res", [P, 2 * P])

        bank = [ctx.enter_context(nc.psum_tensor(f"bank{i}", [P, BLK], F32)) for i in range(8)]

        in_win, in_wout, in_bw, in_cst, in_gate = (sem(n) for n in ("in_win", "in_wout", "in_bw", "in_cst", "in_gate"))
        in_x = [sem(f"in_x{n}") for n in range(NBLK)]
        in_fwd, in_neg, in_inv, in_bins = sem("in_fwd"), sem("in_neg"), sem("in_inv"), sem("in_bins")
        in_w1, in_w2, in_w3 = sem("in_w1"), sem("in_w2"), sem("in_w3")
        zeroed, eps_set = sem("zeroed"), sem("eps_set")
        dve_own, pool_own = sem("dve_own"), sem("pool_own")
        id16_set, bw_set = sem("id16_set"), sem("bw_set")
        wsplit = sem("wsplit")
        gate_set = sem("gate_set")
        c_done, sq_done, v_done, std_done, rstd_done, ln_done, xy_done = (
            sem(n) for n in ("c_done", "sq_done", "v_done", "std_done", "rstd_done", "ln_done", "xy_done"))
        proj_done, lower_out, fold_done, dft_done, gain_done = (
            sem(n) for n in ("proj_done", "lower_out", "fold_done", "dft_done", "gain_done"))
        pow_a, pow_sum, mag_done, filt_done, filt_tp, filt_to, inv_done = (
            sem(n) for n in ("pow_a", "pow_sum", "mag_done", "filt_done", "filt_tp", "filt_to", "inv_done"))
        odd_out, enh_done, outp_done, x1_done = (sem(n) for n in ("odd_out", "enh_done", "outp_done", "x1_done"))
        cen_ps, cen_done, censq_done, ssq_done, stdt_done, rstdt_done = (
            sem(n) for n in ("cen_ps", "cen_done", "censq_done", "ssq_done", "stdt_done", "rstdt_done"))
        tok_done, hi_done, hi2_done, lo_done, xab_ps, xab_done = (
            sem(n) for n in ("tok_done", "hi_done", "hi2_done", "lo_done", "xab_ps", "xab_done"))
        in_xc = [sem(f"in_xc{k}") for k in range(2)]
        lg_done, gap_done, ratio_done, disp_done = (sem(n) for n in ("lg_done", "gap_done", "ratio_done", "disp_done"))
        h_done, silu_done, hid_done, down_done, prod_done, acc_done, ffn_done, fin_done, res_done, stored = (
            sem(n) for n in ("h_done", "silu_done", "hid_done", "down_done", "prod_done", "acc_done", "ffn_done",
                             "fin_done", "res_done", "stored"))

        x_v = x.rearrange("(g h) c a b -> (h c) g (a b)", h=2)
        out_v = out.rearrange("(g h) c a b -> (h c) g (a b)", h=2)
        ln_q = ln[:, :].rearrange("p (n q m) -> p n q m", n=NBLK, q=2)

        def by_quadrants(block):
            return block.rearrange("p (x q y) -> p q x y", q=2, y=16)
        xs_v = xs[:, :].rearrange("p (g x y) -> p g x y", g=G, x=H)

        block = ctx.enter_context(nc.Block())

        @block.sync
        def _(sp):
            for n in range(NBLK):
                sp.dma_start(xs[:, n * BLK:(n + 1) * BLK], x_v[:, n // 2, (n % 2) * BLK:(n % 2 + 1) * BLK]).then_inc(in_x[n], 16)
            for n, (w, raw) in enumerate(((w1, w1_raw), (w2, w2_raw))):
                for h in range(2):
                    sp.dma_start(raw[h * C:(h + 1) * C, :, :], w).then_inc((in_w1, in_w2)[n], 16)
            sp.dma_start(w3_sb[:, :, :], w3).then_inc(in_w3, 16)
            def load(c, k):
                sp.dma_start(xc[:, k, :, :], xab[:, bass.ds(c, 1), :, :].rearrange("p o a n -> p (o a) n")).then_inc(in_xc[k], 16)

            def store(c):
                sp.wait_ge(res_done, c + 1)
                g, q = c // (PIX // (2 * P)), c % (PIX // (2 * P))
                dst = out_v[:, bass.ds(g, 1), bass.ds(q * (2 * P), 2 * P)].rearrange("p o n -> p (o n)")
                sp.dma_start(dst, res[:, :]).then_inc(stored, 16)

            sp.wait_ge(xab_done, CHUNKS)
            load(0, 0)
            load(1, 1)

            def chunk(c, k, _):
                if not first_chunk(c):
                    if not last_chunk(c):
                        sp.wait_ge(h_done, E * c)
                        load(c + 1, 1 - k)
                    store(c - 1)

            over_chunks(sp, chunk)
            store(CHUNKS - 1)
            sp.wait_ge(stored, 16 * CHUNKS)

        @block.scalar
        def _(act):
            act.dma_start(cst[:, :], t_const).then_inc(in_cst, 16)
            act.wait_ge(zeroed, 1)
            for h in range(2):
                act.dma_start(w_in_bd[h * C:(h + 1) * C, h * M:(h + 1) * M], w_in).then_inc(in_win, 16)
            act.dma_start(bw_rows[:, :], bin_w).then_inc(in_bw, 16)
            act.dma_start(fwd, t_fwd.rearrange("p (k c n) -> p k c n", k=KT, c=4)).then_inc(in_fwd, 16)
            act.dma_start(neg, t_neg.rearrange("p (k c n) -> p k c n", k=KT, c=4)).then_inc(in_neg, 16)
            act.dma_start(bins, t_bins).then_inc(in_bins, 16)
            act.dma_start(inv, t_inv.rearrange("p (k c n) -> p k c n", k=KT, c=4)).then_inc(in_inv, 16)
            for gh in range(B):
                act.dma_start(w_out_bd[gh * M:(gh + 1) * M, gh % 2 * C:(gh % 2 + 1) * C], w_out).then_inc(in_wout, 16)
            for h in range(2):
                act.dma_start(gate_raw[h * C:(h + 1) * C, :], gate_w).then_inc(in_gate, 16)
            act.dma_start(gate_b_all[:, :], gate_b.rearrange("(o e) -> o e", o=1).to_broadcast([P, E])).then_inc(in_gate, 16)

            def deviation(n):
                act.wait_ge(v_done, n + 1)
                if n == 0:
                    act.wait_ge(eps_set, 2)
                if n >= 2:
                    act.wait_ge(rstd_done, n - 1)
                nc.scalar.activation(std[:, n % 2, :], bank[6 + n % 2][:, :], ACT.Sqrt, bias=eps_conv[:, :]).then_inc(std_done, 1)

            for n in range(NBLK):
                act.wait_ge(c_done, n + 1)
                if n >= 2:
                    act.wait_ge(v_done, n - 1)
                nc.scalar.activation(sq[:, n % 2, :], bank[n % 4][:, :], ACT.Square).then_inc(sq_done, 1)
                if n >= 1:
                    deviation(n - 1)
            deviation(NBLK - 1)

            act.wait_ge(proj_done, NBLK)
            nc.scalar.copy(half_b[:, :], bank[5][:, :]).then_inc(lower_out, 1)
            for k in range(2):
                act.wait_ge(dft_done, k + 1)
                nc.scalar.activation(power[:, k, 0, :], bank[k][:, :], ACT.Square)
                nc.scalar.activation(power[:, k, 1, :], bank[2 + k][:, :], ACT.Square).then_inc(pow_a, 1)
            for k in range(2):
                act.wait_ge(pow_sum, k + 1)
                nc.scalar.activation(mag[:, k, :], pwc[:, k, :], ACT.Sqrt, scale=0.5).then_inc(mag_done, 1)
            for k in range(2):
                act.wait_ge(filt_tp, k + 1)
                nc.scalar.copy(filt_t[:, 2 * k:2 * k + 2, :, :], bank[4 + k][:, :].rearrange("p (c k n) -> p c k n", c=2, k=KT)).then_inc(filt_to, 1)
            act.wait_ge(inv_done, 2)
            nc.scalar.copy(half_b[:, :], bank[1][:, :]).then_inc(odd_out, 1)

            for n in range(NBLK):
                act.wait_ge(cen_ps, n + 1)
                if n >= 2:
                    act.wait_ge(ssq_done, n - 1)
                nc.scalar.activation(cen_sq[:, n % 2, :], bank[n % 4][:, :], ACT.Square).then_inc(censq_done, 1)
            act.wait_ge(ssq_done, NBLK)
            nc.scalar.activation(std_t[:, :], ssq[:, :], ACT.Sqrt, bias=eps_ffn[:, :], scale=1.0 / C).then_inc(stdt_done, 1)

            def transposed_out(c):
                act.wait_ge(xab_ps, c + 1)
                nc.scalar.copy(xab[:, c, :, :], bank[c % 2][:, :].bitcast(F16).rearrange("p (a n) -> p a n", a=2)).then_inc(xab_done, 1)

            for c in range(CHUNKS):
                act.wait_ge(tok_done, c + 1)
                if c >= 2:
                    act.wait_ge(xab_ps, c - 1)
                nc.scalar.copy(parts[:, c % 2, :, 0, :], tok[:, c % 2, :, :]).then_inc(hi_done, 1)
                if c >= 1:
                    transposed_out(c - 1)
            transposed_out(CHUNKS - 1)
            act.wait_ge(gap_done, 1)
            nc.scalar.activation(ratio[:, :], gap[:, :], ACT.Exp).then_inc(ratio_done, 1)

            def chunk(c, k, load):
                for e in range(E):
                    n = E * c + e
                    act.wait_ge(h_done, n + 1)
                    wait_past(act, hid_done, n - 1)
                    nc.scalar.activation(gated[:, e % 2, :], bank[e % 2][:, :], ACT.Silu, scale=1.0 / WSCALE).then_inc(silu_done, 1)

            over_chunks(act, chunk)

        @block.tensor
        def _(pe):
            pe.wait_ge(in_cst, 16)
            def variance(n):
                pe.wait_ge(sq_done, n + 1)
                if n >= 2:
                    pe.wait_ge(std_done, n - 1)
                nc.tensor.matmul(bank[6 + n % 2][:, :], mean64, sq[:, n % 2, :], start=True, stop=True).then_inc(v_done, 1)

            for n in range(NBLK):
                pe.wait_ge(in_x[n], 16)
                if n >= 4:
                    pe.wait_ge(ln_done, n - 3)
                nc.tensor.matmul(bank[n % 4][:, :], centre, xs[:, n * BLK:(n + 1) * BLK], start=True, stop=True).then_inc(c_done, 1)
                if n >= 1:
                    variance(n - 1)
            variance(NBLK - 1)

            pe.wait_ge(in_win, 16 * 2)
            for n in range(NBLK):
                g, qx = n // 2, n % 2
                pe.wait_ge(ln_done, n + 1)
                for qy in range(2):
                    for kt in range(KT):
                        col = (qy * KT + kt) * P + g * 2 * M
                        last = nc.tensor.matmul(bank[4 + qx][:, col:col + 2 * M], ln_q[:, n, qy, kt * P:(kt + 1) * P],
                                                w_in_bd[:, :], start=True, stop=True)
                last.then_inc(proj_done, 1)

            pe.wait_ge(bw_set, 1)
            pe.wait_ge(in_bins, 16)
            pe.wait_ge(std_done, NBLK)
            for k in range(2):
                last = nc.tensor.matmul(bank[6 + k][:, :], bw_cols[:, :, :].rearrange("a b m -> a (b m)"),
                                        bins[:, k * BLK:(k + 1) * BLK], start=True, stop=True)
            last.then_inc(gain_done, 1)

            pe.wait_ge(in_fwd, 16)
            pe.wait_ge(in_neg, 16)
            pe.wait_ge(fold_done, 1)
            for cls in range(4):
                for table, first_bank in ((fwd, 0), (neg, 2)):
                    dst = bank[first_bank + cls // 2][:, (cls % 2) * QPIX:(cls % 2 + 1) * QPIX]
                    for kt in range(KT):
                        last = nc.tensor.matmul(dst, fold2[:, cls, kt * P:(kt + 1) * P], table[:, kt, cls, :],
                                                start=(kt == 0), stop=(kt == KT - 1))
                if cls % 2:
                    last.then_inc(dft_done, 1)

            for cls in range(4):
                if cls % 2 == 0:
                    pe.wait_ge(filt_done, cls // 2 + 1)
                for kt in range(KT):
                    col = ((cls % 2) * KT + kt) * P
                    last = nc.tensor.transpose(bank[4 + cls // 2][:, col:col + P], filt[:, cls, kt * P:(kt + 1) * P], ident)
                if cls % 2:
                    last.then_inc(filt_tp, 1)
            pe.wait_ge(in_inv, 16)
            for cls in range(4):
                if cls % 2 == 0:
                    pe.wait_ge(filt_to, cls // 2 + 1)
                for kt in range(KT):
                    last = nc.tensor.matmul(bank[cls // 2][:, (cls % 2) * QPIX:(cls % 2 + 1) * QPIX], filt_t[:, cls, kt, :],
                                            inv[:, kt, cls, :], start=(kt == 0), stop=(kt == KT - 1))
                if cls % 2:
                    last.then_inc(inv_done, 1)

            pe.wait_ge(in_wout, 16 * B)
            pe.wait_ge(enh_done, 1)
            for qx in range(2):
                for g in range(G):
                    rows = slice(2 * M * g, 2 * M * (g + 1))
                    last = nc.tensor.matmul(bank[(2 + 4 * qx + g) % 8][:, :], w_out_bd[rows, :],
                                            enh[rows, 2 * qx:2 * qx + 2, :], start=True, stop=True)
                    last.then_inc(outp_done, 1)

            for n in range(NBLK):
                pe.wait_ge(x1_done, 2 * G)
                if n >= 4:
                    pe.wait_ge(cen_done, n - 3)
                    pe.wait_ge(censq_done, n - 3)
                for k in range(4):
                    col = n * BLK + k * P
                    last = nc.tensor.matmul(bank[n % 4][:, k * P:(k + 1) * P], xs[:, col:col + P], centre, start=True, stop=True)
                last.then_inc(cen_ps, 1)

            pe.wait_ge(cen_done, NBLK)
            pe.wait_ge(censq_done, NBLK)
            pe.wait_ge(id16_set, 1)
            pe.wait_ge(gate_set, 1)

            def logits(c):
                pe.wait_ge(xab_done, c + 1)
                for s in range(SUB):
                    t = c * SUB + s
                    dst = bank[4 + t * E // BLK][:, t * E % BLK:t * E % BLK + E]
                    lhs = xab[:, c, 0, s * P:(s + 1) * P]
                    nc.tensor.matmul(dst, lhs, gate_hi[:, :], start=True, stop=False)
                    last = nc.tensor.matmul(dst, lhs, gate_lo[:, :], start=False, stop=True)
                last.then_inc(lg_done, 1)

            for c in range(CHUNKS):
                pe.wait_ge(lo_done, c + 1)
                pe.wait_ge(hi2_done, c + 1)
                if c >= 2:
                    pe.wait_ge(xab_done, c - 1)
                dst = bank[c % 2][:, :].bitcast(F16).rearrange("p (a n) -> p a n", a=2)
                for s in range(SUB):
                    for a in range(2):
                        last = nc.tensor.transpose(dst[:, a, s * P:(s + 1) * P],
                                                   parts[:, c % 2, s, a:a + 2, :].rearrange("p a c -> p (a c)"), ident16[:, :])
                last.then_inc(xab_ps, 1)
                if c >= 1:
                    logits(c - 1)
            logits(CHUNKS - 1)

            pe.wait_ge(wsplit, 2)
            pe.wait_ge(in_w3, 16)
            pe.wait_ge(disp_done, 1)

            def down(c, e):
                n = E * c + e
                pe.wait_ge(hid_done, n + 1)
                if e % 2 == 0:
                    wait_past(pe, prod_done, PAIRS * c + e // 2 - 1)
                for s in range(SUB):
                    col = (s * 2 + e % 2) * C
                    last = nc.tensor.matmul(bank[4 + e // 2 % 2][:, col:col + C], hid[:, e % 2, s * P:(s + 1) * P],
                                            w3_sb[:, e, :], start=True, stop=True)
                last.then_inc(down_done, 1)

            def back_to_channels(c):
                pe.wait_ge(ffn_done, c + 1)
                wait_past(pe, res_done, c)
                for j in range(2):
                    last = nc.tensor.transpose(bank[6][:, j * P:(j + 1) * P],
                                               ffn[:, 2 * j:2 * j + 2, :].rearrange("p h c -> p (h c)"), ident)
                last.then_inc(fin_done, 1)

            def chunk(c, k, load):
                pe.wait_ge(in_xc[k], 16 * load)
                xa, xb = xc[:, k, 0, :], xc[:, k, 1, :]
                for e in range(E):
                    n = E * c + e
                    h1, h2 = bank[e % 2][:, :], bank[2 + e % 2][:, :]
                    wait_past(pe, silu_done, n - 1)
                    wait_past(pe, hid_done, n - 1)
                    nc.tensor.matmul(h1, w1_hi[:, e, :], xa, start=True, stop=False)
                    nc.tensor.matmul(h2, w2_hi[:, e, :], xa, start=True, stop=False)
                    nc.tensor.matmul(h1, w12_lo[0:C, e, :], xa[0:C, :], start=False, stop=True)
                    nc.tensor.matmul(h2, w12_lo[C:P, e, :], xb[C:P, :], start=False, stop=True).then_inc(h_done, 1)
                    if e >= 1:
                        down(c, e - 1)
                    elif not first_chunk(c):
                        down(c - 1, E - 1)
                    if e == FIN_AT and not first_chunk(c):
                        back_to_channels(c - 1)

            over_chunks(pe, chunk)
            down(CHUNKS - 1, E - 1)
            back_to_channels(CHUNKS - 1)

        @block.vector
        def _(dve):
            own = [0]

            def step(ins):
                own[0] += 1
                ins.then_inc(dve_own, 1)
                dve.wait_ge(dve_own, own[0])

            nc.vector.memset(w_in_bd[:, :], 0.0)
            nc.vector.memset(w_out_bd[:, :], 0.0).then_inc(zeroed, 1)
            nc.vector.memset(eps_conv[:, :], EPS_CONV_LN).then_inc(eps_set, 1)
            nc.vector.memset(eps_ffn[:, :], EPS_FFN_LN).then_inc(eps_set, 1)
            dve.wait_ge(in_cst, 16)
            nc.vector.tensor_copy(ident16[:, :], ident).then_inc(id16_set, 1)
            dve.wait_ge(in_bw, 16)
            nc.vector.tensor_copy(bw_cols[:, :, :], bw_rows[:, :].unsqueeze(1).to_broadcast([AR, B, M])).then_inc(bw_set, 1)

            for n in range(NBLK):
                dve.wait_ge(std_done, n + 1)
                nc.vector.reciprocal(rstd[:, n % 2, :], std[:, n % 2, :]).then_inc(rstd_done, 1)
                dve.wait_ge(rstd_done, n + 1)
                nc.vector.tensor_tensor(ln_q[:, n, :, :].rearrange("p q (x y) -> p q x y", y=16), by_quadrants(bank[n % 4][:, :]),
                                        by_quadrants(rstd[:, n % 2, :]), ALU.mult).then_inc(ln_done, 1)

            def butterfly(out_tile, upper, lower):
                up, low = (t.rearrange("p (q n) -> p q n", q=2) for t in (upper, lower))
                nc.vector.tensor_tensor(fold1[:, 0, :, :], up, low, ALU.add)
                step(nc.vector.tensor_tensor(fold1[:, 1, :, :], up, low, ALU.subtract))
                pairs = out_tile.rearrange("p (a b) n -> p a b n", a=2)
                nc.vector.tensor_tensor(pairs[:, :, 0, :], fold1[:, :, 0, :], fold1[:, :, 1, :], ALU.add)
                return nc.vector.tensor_tensor(pairs[:, :, 1, :], fold1[:, :, 0, :], fold1[:, :, 1, :], ALU.subtract)

            dve.wait_ge(proj_done, NBLK)
            dve.wait_ge(lower_out, 1)
            butterfly(fold2[:, :, :], bank[4][:, :], half_b[:, :]).then_inc(fold_done, 1)

            for k in range(2):
                dve.wait_ge(pow_a, k + 1)
                step(nc.vector.tensor_tensor(pw[:, k, :], power[:, k, 0, :], power[:, k, 1, :], ALU.add))
                nc.vector.tensor_scalar(pwc[:, k, :], pw[:, k, :], 2 * SQRT_MIN, None, ALU.max).then_inc(pow_sum, 1)
            dve.wait_ge(gain_done, 1)
            for k in range(2):
                dve.wait_ge(mag_done, k + 1)
                step(nc.vector.reciprocal(rmag[:, k, :], mag[:, k, :]))
                step(nc.vector.tensor_tensor(unit[:, k, :], bank[k][:, :], rmag[:, k, :], ALU.mult))
                step(nc.vector.scalar_tensor_tensor(unit1[:, k, :], pw[:, k, :], 0.0, unit[:, k, :], ALU.is_equal, ALU.add))
                step(nc.vector.scalar_tensor_tensor(zed[:, k, :], unit1[:, k, :], EPS_MAG, bank[k][:, :], ALU.mult, ALU.add))
                nc.vector.tensor_tensor(filt[:, 2 * k:2 * k + 2, :].rearrange("p c n -> p (c n)"), zed[:, k, :], bank[6 + k][:, :],
                                        ALU.mult).then_inc(filt_done, 1)
            dve.wait_ge(inv_done, 2)
            dve.wait_ge(odd_out, 1)
            butterfly(enh[:, :, :], bank[0][:, :], half_b[:, :]).then_inc(enh_done, 1)

            for qx in range(2):
                for g in range(G):
                    idx = qx * G + g
                    dve.wait_ge(outp_done, idx + 1)
                    dve.wait_ge(xy_done, 2 * g + qx + 1)
                    dst = xs_v[:, g, 16 * qx:16 * qx + 16, :].rearrange("p x (q y) -> p q x y", q=2)
                    src = bank[(2 + idx) % 8][:, :].rearrange("p (q x y) -> p q x y", q=2, x=16)
                    nc.vector.tensor_tensor(dst, src, dst, ALU.add).then_inc(x1_done, 1)

            for n in range(NBLK):
                dve.wait_ge(censq_done, n + 1)
                nc.vector.tensor_copy(cen[:, 8 * n:8 * n + 8, :].rearrange("p t c -> p (t c)"), bank[n % 4][:, :]).then_inc(cen_done, 1)
                nc.vector.tensor_reduce(ssq[:, 8 * n:8 * n + 8], cen_sq[:, n % 2, :].rearrange("p (t c) -> p t c", t=8),
                                        AX_X, ALU.add).then_inc(ssq_done, 1)
            dve.wait_ge(stdt_done, 1)
            nc.vector.reciprocal(rstd_t[:, :], std_t[:, :]).then_inc(rstdt_done, 1)
            dve.wait_ge(rstdt_done, 1)

            def low_part(c):
                dve.wait_ge(hi_done, c + 1)
                if c >= 2:
                    dve.wait_ge(xab_ps, c - 1)
                nc.vector.tensor_tensor(parts[:, c % 2, :, 1, :], tok[:, c % 2, :, :], parts[:, c % 2, :, 0, :],
                                        ALU.subtract).then_inc(lo_done, 1)

            for c in range(CHUNKS):
                if c >= 2:
                    dve.wait_ge(lo_done, c - 1)
                nc.vector.tensor_tensor(tok[:, c % 2, :, :], cen[:, SUB * c:SUB * (c + 1), :],
                                        rstd_t[:, SUB * c:SUB * (c + 1)].unsqueeze(2).to_broadcast([P, SUB, C]),
                                        ALU.mult).then_inc(tok_done, 1)
                if c >= 1:
                    low_part(c - 1)
            low_part(CHUNKS - 1)

            dve.wait_ge(lg_done, CHUNKS)
            dve.wait_ge(in_gate, 16 * 3)
            half = TILES // 2
            for k in range(2):
                last = nc.vector.scalar_tensor_tensor(lg[:, k * half:(k + 1) * half, :],
                                                      bank[4 + k][:, :].rearrange("p (t e) -> p t e", e=E), 1.0 / WSCALE,
                                                      gate_b_all[:, :].unsqueeze(1).to_broadcast([P, half, E]), ALU.mult, ALU.add)
            step(last)

            def over_experts(t):
                return t.unsqueeze(2).to_broadcast([P, TILES, E])

            def first_of_largest(onehot, logit, largest):
                step(nc.vector.tensor_reduce(largest[:, :], logit[:, :, :], AX_X, ALU.max))
                step(nc.vector.tensor_tensor(cand[:, :, :], logit[:, :, :], over_experts(largest[:, :]), ALU.is_equal))
                step(nc.vector.tensor_tensor(cand[:, :, :], cand[:, :, :], rev_iota.unsqueeze(1).to_broadcast([P, TILES, E]), ALU.mult))
                step(nc.vector.tensor_reduce(top[:, :], cand[:, :, :], AX_X, ALU.max))
                step(nc.vector.tensor_tensor(onehot[:, :, :], cand[:, :, :], over_experts(top[:, :]), ALU.is_equal))

            first_of_largest(first, lg, m1)
            step(nc.vector.scalar_tensor_tensor(lg2[:, :, :], first[:, :, :], -FAR, lg[:, :, :], ALU.mult, ALU.add))
            first_of_largest(second, lg2, m2)
            nc.vector.tensor_tensor(gap[:, :], m2[:, :], m1[:, :], ALU.subtract).then_inc(gap_done, 1)
            dve.wait_ge(ratio_done, 1)
            step(nc.vector.tensor_scalar(wt2[:, :], ratio[:, :], 1.0, WSCALE, ALU.add, ALU.mult))
            step(nc.vector.reciprocal(wt1[:, :], wt2[:, :]))
            step(nc.vector.tensor_tensor(wt2[:, :], wt1[:, :], ratio[:, :], ALU.mult))
            step(nc.vector.tensor_tensor(first[:, :, :], first[:, :, :], over_experts(wt1[:, :]), ALU.mult))
            step(nc.vector.tensor_tensor(second[:, :, :], second[:, :, :], over_experts(wt2[:, :]), ALU.mult))
            step(nc.vector.tensor_tensor(disp[:, :, :], first[:, :, :], second[:, :, :], ALU.add))
            dve.sem_inc(disp_done, 1)

            def weigh(c, m):
                dve.wait_ge(down_done, E * c + 2 * m + 2)
                src = bank[4 + m % 2][:, :].rearrange("p (s e c) -> p s e c", s=SUB, e=2)
                wt = disp[:, bass.ds(SUB * c, SUB), 2 * m:2 * m + 2].unsqueeze(3).to_broadcast([P, SUB, 2, C])
                if m == 0:
                    wait_past(dve, ffn_done, c)
                    dst = acc[:, :, :, :]
                else:
                    wait_past(dve, acc_done, (PAIRS - 1) * c + (m - 2 if m >= 3 else 1 - m))
                    dst = prod[:, m % 2, :, :, :]
                nc.vector.tensor_tensor(dst, src, wt, ALU.mult).then_inc(prod_done, 1)

            def result(c):
                dve.wait_ge(fin_done, c + 1)
                wait_past(dve, stored, 16 * c)
                nc.vector.tensor_tensor(res[:, :], bank[6][:, 0:2 * P], xs[:, bass.ds(2 * P * c, 2 * P)], ALU.add).then_inc(res_done, 1)

            def chunk(c, k, load):
                for e in range(E):
                    n = E * c + e
                    dve.wait_ge(silu_done, n + 1)
                    wait_past(dve, down_done, n - 1)
                    nc.vector.tensor_tensor(hid[:, e % 2, :], bank[2 + e % 2][:, :], gated[:, e % 2, :], ALU.mult).then_inc(hid_done, 1)
                    if e % 2 == 0:
                        if e >= 2:
                            weigh(c, e // 2 - 1)
                        elif not first_chunk(c):
                            weigh(c - 1, PAIRS - 1)
                    if e == FIN_AT + 1 and not first_chunk(c):
                        result(c - 1)

            over_chunks(dve, chunk)
            weigh(CHUNKS - 1, PAIRS - 1)
            result(CHUNKS - 1)

        @block.gpsimd
        def _(pool):
            pool.wait_ge(in_gate, 16 * 3)
            nc.gpsimd.tensor_scalar(gate_raw[:, :], gate_raw[:, :], WSCALE, None, ALU.mult).then_inc(pool_own, 1)
            pool.wait_ge(pool_own, 1)
            nc.gpsimd.tensor_copy(gate_hi[:, :], gate_raw[:, :]).then_inc(pool_own, 1)
            pool.wait_ge(pool_own, 2)
            nc.gpsimd.tensor_tensor(gate_lo[:, :], gate_raw[:, :], gate_hi[:, :], ALU.subtract).then_inc(gate_set, 1)
            for n in range(NBLK):
                pool.wait_ge(ln_done, n + 1)
                cols = slice(n * BLK, (n + 1) * BLK)
                nc.gpsimd.tensor_tensor(by_quadrants(xs[:, cols]), by_quadrants(xs[:, cols]),
                                        ln_q[:, n, :, :].rearrange("p q (x y) -> p q x y", y=16), ALU.add).then_inc(xy_done, 1)
            for n, (raw, hi, rows, loaded) in enumerate(((w1_raw, w1_hi, slice(0, C), in_w1), (w2_raw, w2_hi, slice(C, P), in_w2))):
                pool.wait_ge(loaded, 16 * 2)
                nc.gpsimd.tensor_scalar(raw[:, :, :], raw[:, :, :], WSCALE, None, ALU.mult).then_inc(pool_own, 1)
                pool.wait_ge(pool_own, 3 + 2 * n)
                nc.gpsimd.tensor_copy(hi[:, :, :], raw[:, :, :]).then_inc(pool_own, 1)
                pool.wait_ge(pool_own, 4 + 2 * n)
                nc.gpsimd.tensor_tensor(w12_lo[rows, :, :], raw[rows, :, :], hi[rows, :, :], ALU.subtract).then_inc(wsplit, 1)

            pool.wait_ge(wsplit, 2)

            for c in range(CHUNKS):
                pool.wait_ge(hi_done, c + 1)
                if c >= 2:
                    pool.wait_ge(xab_ps, c - 1)
                nc.gpsimd.tensor_copy(parts[:, c % 2, :, 2, :].bitcast(F32), parts[:, c % 2, :, 0, :].bitcast(F32)).then_inc(hi2_done, 1)

            def chunk(c, k, load):
                for m in range(1, PAIRS):
                    pool.wait_ge(prod_done, PAIRS * c + m + 1)
                    wait_past(pool, acc_done, (PAIRS - 1) * c + m - 1)
                    nc.gpsimd.tensor_tensor(acc[:, :, :, :], acc[:, :, :, :], prod[:, m % 2, :, :, :], ALU.add).then_inc(acc_done, 1)
                pool.wait_ge(acc_done, (PAIRS - 1) * (c + 1))
                wait_past(pool, fin_done, c)
                nc.gpsimd.tensor_tensor(ffn[:, :, :], acc[:, :, 0, :], acc[:, :, 1, :], ALU.add).then_inc(ffn_done, 1)

            over_chunks(pool, chunk)


_INS = ["x", "L0_conv_w_in", "L0_conv_w_out", "L0_conv_bin_weights", "L0_ffn_gate_w", "L0_ffn_gate_b",
        "L0_ffn_w1", "L0_ffn_w2", "L0_ffn_w3"]


def kernel(**inputs):
    import concourse.bacc as bacc
    from concourse.bass_utils import run_bass_kernel_spmd

    nc = bacc.Bacc("TRN2", target_bir_lowering=False, num_devices=1)
    fwd, neg, inv = hartley_tables()
    tables = {"t_const": constant_tile(), "t_fwd": fwd, "t_neg": neg, "t_inv": inv, "t_bins": bin_table()}
    laid_out = {n: np.asarray(inputs[n]) for n in _INS}
    laid_out["L0_conv_w_in"] = laid_out["L0_conv_w_in"].T
    laid_out["L0_conv_w_out"] = laid_out["L0_conv_w_out"].T
    laid_out["L0_conv_bin_weights"] = laid_out["L0_conv_bin_weights"].reshape(M, AR).T
    for n in ("L0_ffn_w1", "L0_ffn_w2", "L0_ffn_w3"):
        laid_out[n] = laid_out[n].transpose(1, 0, 2)
    arrays, args = {}, []
    for name, a in list(laid_out.items()) + list(tables.items()):
        a = np.ascontiguousarray(a)
        arrays[f"in_{name}"] = a
        args.append(nc.dram_tensor(f"in_{name}", a.shape, mybir.dt.from_np(a.dtype), kind="ExternalInput").ap())
    args.append(nc.dram_tensor("out", (B, C, H, W), F32, kind="ExternalOutput").ap())
    build(nc, *args)
    r = run_bass_kernel_spmd(nc, [arrays], core_ids=[0])
    return r.results[0]["out"]
```

```python
from contextlib import ExitStack

import numpy as np

import concourse.bass as bass
from concourse import mybir

F32 = mybir.dt.float32
F16 = mybir.dt.float16
BF16 = mybir.dt.bfloat16
ALU = mybir.AluOpType
ACT = mybir.ActivationFunctionType
AX_X = mybir.AxisListType.X

B, C, H, W = 8, 64, 32, 32
M = 16
N_ANGLES, RADIUS_WIDTH, OVERLAP = 8, 8, 1.5
N_RADII = max(H // 2, W // 2) // RADIUS_WIDTH + 1
AR = N_ANGLES * N_RADII
E, HID = 16, 128
P = 128
G = B // 2
PIX = H * W
COLS = G * PIX
BLK = 512
NBLK = COLS // BLK
QUADS, KT, QPIX = 4, 2, PIX // 4
CHUNKS = 16
TOK = COLS * 2 // CHUNKS
SUB = TOK // P
TILES = CHUNKS * SUB
EPS_CONV_LN, EPS_FFN_LN, EPS_MAG = 1e-6, 1e-5, 1e-8
SQRT_MIN = 2.0 ** -116
WSCALE = 64.0
HSCALE = 8.0
FAR = 1e30
DPARTS = 3
LO_LAG, DOWN_LAG = 1, 4
SLOTS = 4


FIN_AT = DOWN_LAG + 3


def first_chunk(c):
    return isinstance(c, int) and c == 0


def wait_past(eng, semaphore, value):
    if not isinstance(value, int) or value > 0:
        eng.wait_ge(semaphore, value)


def over_chunks(eng, chunk):
    chunk(0)
    with eng.Fori(1, CHUNKS) as c:
        chunk(c)


def before(c, e, lag):
    if e >= lag:
        return c, e - lag
    return None if first_chunk(c) else (c - 1, e - lag + E)


def hartley_tables():
    xy = np.arange(QPIX)
    x, y = xy // 16, xy % 16
    out = []
    for sign in (1.0, -1.0):
        t = np.empty((QPIX, 4, QPIX))
        for cls in range(4):
            u, v = 2 * x + cls // 2, 2 * y + cls % 2
            th = 2 * np.pi * ((np.outer(x, u) + np.outer(y, v)) % 32) / 32
            t[:, cls] = (np.cos(th) + sign * np.sin(th)) / 32
        out.append(t)
    fwd, neg = out
    inv = fwd.transpose(2, 1, 0)
    tile = lambda t: np.ascontiguousarray(t.reshape(KT, P, 4, QPIX).transpose(1, 0, 2, 3).reshape(P, -1).astype(np.float32))
    return tile(fwd), tile(neg), tile(inv)


def bin_table():
    f = np.float32
    y = np.arange(H, dtype=f)[:, None] - f(H // 2)
    x = np.arange(W, dtype=f)[None, :] - f(W // 2)
    r = np.sqrt(y * y + x * x)
    theta = (np.arctan2(y, x) + f(np.pi)) % f(np.pi)
    ridx = np.clip(np.floor(r / f(RADIUS_WIDTH)).astype(np.int32), 0, N_RADII - 1)
    delta = np.pi / N_ANGLES
    half = OVERLAP * delta / 2.0
    centers = (np.arange(N_ANGLES, dtype=f) * f(delta) + f(delta / 2.0))[:, None, None]
    dist = np.abs(theta[None] - centers)
    w = np.clip(f(1.0) - dist / f(half), f(0.0), None) * (dist < f(half))
    w = w / (w.sum(axis=0, keepdims=True) + f(1e-8))
    full = w[:, None] * (ridx[None, None] == np.arange(N_RADII)[None, :, None, None])
    full = np.fft.ifftshift(full.astype(np.float64), axes=(-2, -1))
    flip = np.roll(full[:, :, ::-1, ::-1], 1, axis=(-2, -1))
    sym = (full + flip) / 2
    a = np.arange(QPIX)
    cols = [sym[:, :, 2 * (a // 16) + cls // 2, 2 * (a % 16) + cls % 2] for cls in range(4)]
    return np.ascontiguousarray(np.stack(cols, 2).reshape(AR, PIX).astype(f))


def constant_tile():
    eye = np.eye(P)
    mean = np.kron(np.eye(2), np.full((C, C), 1.0 / C))
    rev = np.broadcast_to(E - np.arange(E), (P, E))
    merge = np.zeros((2, C, 2, 2, C))
    for h in range(2):
        merge[:, np.arange(C), h, h, np.arange(C)] = 1
    return np.ascontiguousarray(np.concatenate([eye, eye - mean, mean, rev, merge.reshape(P, 2 * P)], 1).astype(np.float32))


def selector_table():
    sel = np.tile(np.eye(E), (DPARTS, 1))[:, :, None]
    return np.ascontiguousarray(np.broadcast_to(sel, (DPARTS * E, E, P)).reshape(DPARTS * E, -1).astype(np.float32))


def build(nc, x, w_in, w_out, bin_w, gate_w, gate_b, w1, w2, w3, t_const, t_fwd, t_neg, t_inv, t_bins, t_sel, out):
    ctx = ExitStack()
    with ctx:
        def sb(name, shape, dt=F32):
            return ctx.enter_context(nc.sbuf_tensor(name, shape, dt))

        def sem(name):
            return ctx.enter_context(nc.semaphore(name))

        cst = sb("cst", [P, 5 * P + E])
        ident, centre, mean64, rev_iota = cst[:, 0:P], cst[:, P:2 * P], cst[:, 2 * P:3 * P], cst[:, 3 * P:3 * P + E]
        merge = cst[:, 3 * P + E:5 * P + E].rearrange("p (h m) -> p h m", h=2)
        ident16 = sb("ident16", [P, P], F16)
        merge16 = sb("merge16", [P, 2, P], F16)
        identb = sb("identb", [P, P], BF16)
        eps_conv, eps_ffn = sb("eps_conv", [P, 1]), sb("eps_ffn", [P, 1])
        w_in_bd = sb("w_in_bd", [P, 2 * M])
        w_out_bd = sb("w_out_bd", [P, P])
        bw_rows = sb("bw_rows", [AR, M])
        bw_cols = sb("bw_cols", [AR, B, M])
        shared = sb("shared", [P, 8, PIX])
        fwd, neg, inv = (shared[:, 2 * n:2 * n + 2, :].rearrange("p k (c n) -> p k c n", c=4) for n in range(3))
        bins = shared[0:AR, 6, :]
        filt_t = shared[:, 7, :].rearrange("p (c k n) -> p c k n", c=4, k=KT)
        xp = shared[:, 0:4, :].rearrange("p a n -> p (a n)").bitcast(F16).rearrange("p (c n) -> p c n", c=CHUNKS)
        dt = shared[0:DPARTS * E, 4:8, :].rearrange("p a n -> p (a n)").bitcast(BF16).rearrange("p (c n) -> p c n", c=CHUNKS)
        gate_raw = sb("gate_raw", [P, E])
        gate_hi, gate_lo = sb("gate_hi", [P, E], F16), sb("gate_lo", [P, E], F16)
        gate_b_all = sb("gate_b_all", [P, E])
        w1_raw, w2_raw = sb("w1_raw", [P, E, HID]), sb("w2_raw", [P, E, HID])
        w1_hi, w2_hi = sb("w1_hi", [P, E, HID], F16), sb("w2_hi", [P, E, HID], F16)
        w1_lo, w2_lo = sb("w1_lo", [P, E, HID], F16), sb("w2_lo", [P, E, HID], F16)
        w3_raw = sb("w3_raw", [P, E, C])
        w3_parts = sb("w3_parts", [P, E, 2, C], F16)
        sel_raw = w1_raw[0:DPARTS * E, :, :]
        sel = sb("sel", [DPARTS * E, E, P], BF16)
        xs = sb("xs", [P, COLS])
        ln = sb("ln", [P, COLS])
        sq = sb("sq", [P, 2, BLK])
        std = sb("std", [P, 2, BLK])
        rstd = sb("rstd", [P, 2, BLK])
        half_b = sb("half_b", [P, BLK])
        fold1 = sb("fold1", [P, 2, 2, QPIX])
        fold2 = sb("fold2", [P, 4, QPIX])
        power = sb("power", [P, 2, 2, BLK])
        pw = sb("pw", [P, 2, BLK])
        pwc = sb("pwc", [P, 2, BLK])
        mag = sb("mag", [P, 2, BLK])
        rmag = sb("rmag", [P, 2, BLK])
        unit = sb("unit", [P, 2, BLK])
        unit1 = sb("unit1", [P, 2, BLK])
        zed = sb("zed", [P, 2, BLK])
        filt = sb("filt", [P, 4, QPIX])
        enh = sb("enh", [P, 4, QPIX])
        cen = ln[:, :].rearrange("p (t c) -> p t c", t=TILES)
        cen_sq = sb("cen_sq", [P, 2, 8 * C])
        ssq = sb("ssq", [P, TILES])
        std_t, rstd_t = sb("std_t", [P, TILES]), sb("rstd_t", [P, TILES])
        tok = sb("tok", [P, 2, SUB, C])
        parts = sb("parts", [P, 2, SUB, 2, C], F16)
        lg, lg2, cand, first, second = (t[:, :, :].rearrange("p k (t e) -> p (k t) e", e=E)
                                        for t in (mag, rmag, unit, unit1, zed))
        m1, m2, top = sb("m1", [P, TILES]), sb("m2", [P, TILES]), sb("top", [P, TILES])
        gap, ratio, wt1, wt2 = (sb(n, [P, TILES]) for n in ("gap", "ratio", "wt1", "wt2"))
        rest = second
        disp = sb("disp", [P, TILES, E])
        disp_parts = sb("disp_parts", [P, TILES, DPARTS, E], BF16)
        gated = fold1[:, :, :, :].rearrange("p a b n -> p a (b n)")
        both = [t[:, k, :] for t in (pw, pwc) for k in range(2)]
        hid = power[:, :, :, :].rearrange("p a b n -> p (a b) n")
        hid_hi, hid_lo = (t[:, :, :].rearrange("p a n -> p (a n)").bitcast(F16).rearrange("p (k n) -> p k n", k=SLOTS)
                          for t in (filt, enh))
        ffn_hi, ffn_lo = sb("ffn_hi", [P, TOK], F16), sb("ffn_lo", [P, TOK], F16)
        res = sb("res", [P, 2 * P])

        bank = [ctx.enter_context(nc.psum_tensor(f"bank{i}", [P, BLK], F32)) for i in range(6)]
        sums = ctx.enter_context(nc.psum_tensor("sums", [P, 2, BLK], F32))
        bank += [sums[:, k, :] for k in range(2)]

        def sum_bank(c):
            return bank[6 + c % 2] if isinstance(c, int) else sums[:, bass.ds(c % 2, 1), :].rearrange("p o n -> p (o n)")

        in_win, in_wout, in_bw, in_cst, in_gate = (sem(n) for n in ("in_win", "in_wout", "in_bw", "in_cst", "in_gate"))
        in_x = [sem(f"in_x{n}") for n in range(NBLK)]
        in_fwd, in_neg, in_inv, in_bins = sem("in_fwd"), sem("in_neg"), sem("in_inv"), sem("in_bins")
        in_w1, in_w2, in_w3 = sem("in_w1"), sem("in_w2"), sem("in_w3")
        zeroed, eps_set = sem("zeroed"), sem("eps_set")
        dve_own, pool_own = sem("dve_own"), sem("pool_own")
        id16_set, bw_set = sem("id16_set"), sem("bw_set")
        wsplit = sem("wsplit")
        gate_set = sem("gate_set")
        c_done, sq_done, v_done, std_done, rstd_done, ln_done, xy_done = (
            sem(n) for n in ("c_done", "sq_done", "v_done", "std_done", "rstd_done", "ln_done", "xy_done"))
        proj_done, lower_out, fold_done, dft_done, gain_done = (
            sem(n) for n in ("proj_done", "lower_out", "fold_done", "dft_done", "gain_done"))
        pow_a, pow_sum, mag_done, filt_done, filt_tp, filt_to, inv_done = (
            sem(n) for n in ("pow_a", "pow_sum", "mag_done", "filt_done", "filt_tp", "filt_to", "inv_done"))
        odd_out, enh_done, outp_done, x1_done = (sem(n) for n in ("odd_out", "enh_done", "outp_done", "x1_done"))
        cen_ps, cen_done, censq_done, ssq_done, stdt_done, rstdt_done = (
            sem(n) for n in ("cen_ps", "cen_done", "censq_done", "ssq_done", "stdt_done", "rstdt_done"))
        tok_done, hi_done, lo_done, xp_ps, xp_done = (sem(n) for n in ("tok_done", "hi_done", "lo_done", "xp_ps", "xp_done"))
        in_sel, sel_set, dt_ps, dt_done = (sem(n) for n in ("in_sel", "sel_set", "dt_ps", "dt_done"))
        lg_done, gap_done, ratio_done, disp_done = (sem(n) for n in ("lg_done", "gap_done", "ratio_done", "disp_done"))
        h1_done, h2_done, bcast_done, silu_done, both_done, hid_done, hidhi_done, hidlo_done = (
            sem(n) for n in ("h1_done", "h2_done", "bcast_done", "silu_done", "both_done", "hid_done", "hidhi_done",
                             "hidlo_done"))
        down_done, ffnhi_done, ffn_done, fin_done, res_done, stored = (
            sem(n) for n in ("down_done", "ffnhi_done", "ffn_done", "fin_done", "res_done", "stored"))

        x_v = x.rearrange("(g h) c a b -> (h c) g (a b)", h=2)
        out_v = out.rearrange("(g h) c a b -> (h c) g (a b)", h=2)
        ln_q = ln[:, :].rearrange("p (n q m) -> p n q m", n=NBLK, q=2)

        def by_quadrants(block):
            return block.rearrange("p (x q y) -> p q x y", q=2, y=16)
        xs_v = xs[:, :].rearrange("p (g x y) -> p g x y", g=G, x=H)

        block = ctx.enter_context(nc.Block())

        @block.sync
        def _(sp):
            for n in range(NBLK):
                sp.dma_start(xs[:, n * BLK:(n + 1) * BLK], x_v[:, n // 2, (n % 2) * BLK:(n % 2 + 1) * BLK]).then_inc(in_x[n], 16)
            for n, (w, raw) in enumerate(((w1, w1_raw), (w2, w2_raw))):
                for h in range(2):
                    sp.dma_start(raw[h * C:(h + 1) * C, :, :], w).then_inc((in_w1, in_w2)[n], 16)
            sp.dma_start(w3_raw[:, :, :], w3).then_inc(in_w3, 16)
            sp.wait_ge(wsplit, 1)
            sp.dma_start(sel_raw, t_sel.rearrange("p (e n) -> p e n", e=E)).then_inc(in_sel, 16)

            def store(c):
                sp.wait_ge(res_done, c + 2)
                g, q = c // (PIX // (2 * P)), c % (PIX // (2 * P))
                dst = out_v[:, bass.ds(g, 1), bass.ds(q * (2 * P), 2 * P)].rearrange("p o n -> p (o n)")
                sp.dma_start(dst, res[:, :]).then_inc(stored, 16)

            with sp.Fori(0, CHUNKS) as c:
                store(c)
            sp.wait_ge(stored, 16 * CHUNKS)

        @block.scalar
        def _(act):
            act.dma_start(cst[:, :], t_const).then_inc(in_cst, 16)
            act.wait_ge(zeroed, 1)
            for h in range(2):
                act.dma_start(w_in_bd[h * C:(h + 1) * C, h * M:(h + 1) * M], w_in).then_inc(in_win, 16)
            act.dma_start(bw_rows[:, :], bin_w).then_inc(in_bw, 16)
            act.dma_start(fwd, t_fwd.rearrange("p (k c n) -> p k c n", k=KT, c=4)).then_inc(in_fwd, 16)
            act.dma_start(neg, t_neg.rearrange("p (k c n) -> p k c n", k=KT, c=4)).then_inc(in_neg, 16)
            act.dma_start(bins, t_bins).then_inc(in_bins, 16)
            act.dma_start(inv, t_inv.rearrange("p (k c n) -> p k c n", k=KT, c=4)).then_inc(in_inv, 16)
            for gh in range(B):
                act.dma_start(w_out_bd[gh * M:(gh + 1) * M, gh % 2 * C:(gh % 2 + 1) * C], w_out).then_inc(in_wout, 16)
            for h in range(2):
                act.dma_start(gate_raw[h * C:(h + 1) * C, :], gate_w).then_inc(in_gate, 16)
            act.dma_start(gate_b_all[:, :], gate_b.rearrange("(o e) -> o e", o=1).to_broadcast([P, E])).then_inc(in_gate, 16)

            def deviation(n):
                act.wait_ge(v_done, n + 1)
                if n == 0:
                    act.wait_ge(eps_set, 2)
                if n >= 2:
                    act.wait_ge(rstd_done, n - 1)
                nc.scalar.activation(std[:, n % 2, :], bank[6 + n % 2][:, :], ACT.Sqrt, bias=eps_conv[:, :]).then_inc(std_done, 1)

            for n in range(NBLK):
                act.wait_ge(c_done, n + 1)
                if n >= 2:
                    act.wait_ge(v_done, n - 1)
                nc.scalar.activation(sq[:, n % 2, :], bank[n % 4][:, :], ACT.Square).then_inc(sq_done, 1)
                if n >= 1:
                    deviation(n - 1)
            deviation(NBLK - 1)

            act.wait_ge(proj_done, NBLK)
            nc.scalar.copy(half_b[:, :], bank[5][:, :]).then_inc(lower_out, 1)
            for k in range(2):
                act.wait_ge(dft_done, k + 1)
                nc.scalar.activation(power[:, k, 0, :], bank[k][:, :], ACT.Square)
                nc.scalar.activation(power[:, k, 1, :], bank[2 + k][:, :], ACT.Square).then_inc(pow_a, 1)
            for k in range(2):
                act.wait_ge(pow_sum, k + 1)
                nc.scalar.activation(mag[:, k, :], pwc[:, k, :], ACT.Sqrt, scale=0.5).then_inc(mag_done, 1)
            for k in range(2):
                act.wait_ge(filt_tp, k + 1)
                nc.scalar.copy(filt_t[:, 2 * k:2 * k + 2, :, :], bank[4 + k][:, :].rearrange("p (c k n) -> p c k n", c=2, k=KT)).then_inc(filt_to, 1)
            act.wait_ge(inv_done, 2)
            nc.scalar.copy(half_b[:, :], bank[1][:, :]).then_inc(odd_out, 1)

            for n in range(NBLK):
                act.wait_ge(cen_ps, n + 1)
                if n >= 2:
                    act.wait_ge(ssq_done, n - 1)
                nc.scalar.activation(cen_sq[:, n % 2, :], bank[n % 4][:, :], ACT.Square).then_inc(censq_done, 1)
            act.wait_ge(ssq_done, NBLK)
            nc.scalar.activation(std_t[:, :], ssq[:, :], ACT.Sqrt, bias=eps_ffn[:, :], scale=1.0 / C).then_inc(stdt_done, 1)

            def transposed_out(c):
                act.wait_ge(xp_ps, c + 1)
                nc.scalar.copy(xp[:, c, :], bank[c % 2][:, 0:TOK // 2].bitcast(F16)).then_inc(xp_done, 1)

            for c in range(CHUNKS):
                act.wait_ge(tok_done, c + 1)
                if c >= 2:
                    act.wait_ge(xp_ps, c - 1)
                nc.scalar.copy(parts[:, c % 2, :, 0, :], tok[:, c % 2, :, :]).then_inc(hi_done, 1)
                if c >= 1:
                    transposed_out(c - 1)
            transposed_out(CHUNKS - 1)
            act.wait_ge(gap_done, 1)
            nc.scalar.activation(ratio[:, :], gap[:, :], ACT.Exp).then_inc(ratio_done, 1)

            def high_part(c, e):
                n = E * c + e
                act.wait_ge(hid_done, n + 1)
                wait_past(act, down_done, n - SLOTS + 1)
                nc.scalar.copy(hid_hi[:, e % SLOTS, :], hid[:, e % SLOTS, :]).then_inc(hidhi_done, 1)

            def chunk_sum(c):
                act.wait_ge(down_done, E * (c + 1))
                wait_past(act, fin_done, c)
                nc.scalar.activation(ffn_hi[:, :], sum_bank(c), ACT.Copy, scale=1.0 / (WSCALE * HSCALE)).then_inc(ffnhi_done, 1)

            def chunk(c):
                for e in range(E):
                    n = E * c + e
                    act.wait_ge(h1_done, n + 1)
                    wait_past(act, both_done, n - 1)
                    nc.scalar.activation(gated[:, e % 2, :], bank[e % 2][:, :], ACT.Silu, scale=1.0 / WSCALE).then_inc(silu_done, 1)
                    if ce := before(c, e, LO_LAG):
                        high_part(*ce)
                    if e == DOWN_LAG and not first_chunk(c):
                        chunk_sum(c - 1)

            over_chunks(act, chunk)
            for e in range(E - LO_LAG, E):
                high_part(CHUNKS - 1, e)
            chunk_sum(CHUNKS - 1)

        @block.tensor
        def _(pe):
            pe.wait_ge(in_cst, 16)
            def variance(n):
                pe.wait_ge(sq_done, n + 1)
                if n >= 2:
                    pe.wait_ge(std_done, n - 1)
                nc.tensor.matmul(bank[6 + n % 2][:, :], mean64, sq[:, n % 2, :], start=True, stop=True).then_inc(v_done, 1)

            for n in range(NBLK):
                pe.wait_ge(in_x[n], 16)
                if n >= 4:
                    pe.wait_ge(ln_done, n - 3)
                nc.tensor.matmul(bank[n % 4][:, :], centre, xs[:, n * BLK:(n + 1) * BLK], start=True, stop=True).then_inc(c_done, 1)
                if n >= 1:
                    variance(n - 1)
            variance(NBLK - 1)

            pe.wait_ge(in_win, 16 * 2)
            for n in range(NBLK):
                g, qx = n // 2, n % 2
                pe.wait_ge(ln_done, n + 1)
                for qy in range(2):
                    for kt in range(KT):
                        col = (qy * KT + kt) * P + g * 2 * M
                        last = nc.tensor.matmul(bank[4 + qx][:, col:col + 2 * M], ln_q[:, n, qy, kt * P:(kt + 1) * P],
                                                w_in_bd[:, :], start=True, stop=True)
                last.then_inc(proj_done, 1)

            pe.wait_ge(bw_set, 1)
            pe.wait_ge(in_bins, 16)
            pe.wait_ge(std_done, NBLK)
            for k in range(2):
                last = nc.tensor.matmul(bank[6 + k][:, :], bw_cols[:, :, :].rearrange("a b m -> a (b m)"),
                                        bins[:, k * BLK:(k + 1) * BLK], start=True, stop=True)
            last.then_inc(gain_done, 1)

            pe.wait_ge(in_fwd, 16)
            pe.wait_ge(in_neg, 16)
            pe.wait_ge(fold_done, 1)
            for cls in range(4):
                for table, first_bank in ((fwd, 0), (neg, 2)):
                    dst = bank[first_bank + cls // 2][:, (cls % 2) * QPIX:(cls % 2 + 1) * QPIX]
                    for kt in range(KT):
                        last = nc.tensor.matmul(dst, fold2[:, cls, kt * P:(kt + 1) * P], table[:, kt, cls, :],
                                                start=(kt == 0), stop=(kt == KT - 1))
                if cls % 2:
                    last.then_inc(dft_done, 1)

            for cls in range(4):
                if cls % 2 == 0:
                    pe.wait_ge(filt_done, cls // 2 + 1)
                for kt in range(KT):
                    col = ((cls % 2) * KT + kt) * P
                    last = nc.tensor.transpose(bank[4 + cls // 2][:, col:col + P], filt[:, cls, kt * P:(kt + 1) * P], ident)
                if cls % 2:
                    last.then_inc(filt_tp, 1)
            pe.wait_ge(in_inv, 16)
            for cls in range(4):
                if cls % 2 == 0:
                    pe.wait_ge(filt_to, cls // 2 + 1)
                for kt in range(KT):
                    last = nc.tensor.matmul(bank[cls // 2][:, (cls % 2) * QPIX:(cls % 2 + 1) * QPIX], filt_t[:, cls, kt, :],
                                            inv[:, kt, cls, :], start=(kt == 0), stop=(kt == KT - 1))
                if cls % 2:
                    last.then_inc(inv_done, 1)

            pe.wait_ge(in_wout, 16 * B)
            pe.wait_ge(enh_done, 1)
            for qx in range(2):
                for g in range(G):
                    rows = slice(2 * M * g, 2 * M * (g + 1))
                    last = nc.tensor.matmul(bank[(2 + 4 * qx + g) % 8][:, :], w_out_bd[rows, :],
                                            enh[rows, 2 * qx:2 * qx + 2, :], start=True, stop=True)
                    last.then_inc(outp_done, 1)

            for n in range(NBLK):
                pe.wait_ge(x1_done, 2 * G)
                if n >= 4:
                    pe.wait_ge(cen_done, n - 3)
                    pe.wait_ge(censq_done, n - 3)
                for k in range(4):
                    col = n * BLK + k * P
                    last = nc.tensor.matmul(bank[n % 4][:, k * P:(k + 1) * P], xs[:, col:col + P], centre, start=True, stop=True)
                last.then_inc(cen_ps, 1)

            pe.wait_ge(cen_done, NBLK)
            pe.wait_ge(id16_set, 1)
            pe.wait_ge(gate_set, 1)

            def logits(c):
                pe.wait_ge(xp_done, c + 1)
                for s in range(SUB):
                    t = c * SUB + s
                    dst = bank[4 + t * E // BLK][:, t * E % BLK:t * E % BLK + E]
                    lhs = xp[:, c, s * P:(s + 1) * P]
                    nc.tensor.matmul(dst, lhs, gate_hi[:, :], start=True, stop=False)
                    last = nc.tensor.matmul(dst, lhs, gate_lo[:, :], start=False, stop=True)
                last.then_inc(lg_done, 1)

            for c in range(CHUNKS):
                pe.wait_ge(lo_done, c + 1)
                if c >= 2:
                    pe.wait_ge(xp_done, c - 1)
                dst = bank[c % 2][:, 0:TOK // 2].bitcast(F16)
                for s in range(SUB):
                    last = nc.tensor.transpose(dst[:, s * P:(s + 1) * P], parts[:, c % 2, s, :, :].rearrange("p a c -> p (a c)"),
                                               ident16[:, :])
                last.then_inc(xp_ps, 1)
                if c >= 1:
                    logits(c - 1)
            logits(CHUNKS - 1)

            pe.wait_ge(disp_done, 1)
            for n in range(CHUNKS // 2):
                if n >= 2:
                    pe.wait_ge(dt_done, n - 1)
                for s in range(2 * SUB):
                    last = nc.tensor.transpose(bank[2 + n % 2][0:DPARTS * E, :].bitcast(BF16)[:, s * P:(s + 1) * P],
                                               disp_parts[:, 2 * SUB * n + s, :, :].rearrange("p a e -> p (a e)"), identb[:, :])
                last.then_inc(dt_ps, 1)

            pe.wait_ge(wsplit, 3)
            pe.wait_ge(sel_set, 1)
            pe.wait_ge(dt_done, CHUNKS // 2)

            def down(c, e, step=None):
                n = E * c + e
                pe.wait_ge(hidhi_done, n + 1)
                if e == 0:
                    wait_past(pe, res_done, c)
                lhs = w3_parts[:, e, :, :].rearrange("p a c -> p (a c)")
                nc.tensor.matmul(sum_bank(c), lhs, hid_hi[:, e % SLOTS, :], start=(e == 0), stop=False)
                pe.wait_ge(hidlo_done, n + 1)
                if step is not None:
                    wait_past(pe, hid_done, step - 1)
                nc.tensor.matmul(sum_bank(c), lhs, hid_lo[:, e % SLOTS, :], start=False, stop=(e == E - 1)).then_inc(down_done, 1)

            def merge_parts(c):
                pe.wait_ge(ffn_done, c + 1)
                for h in range(2):
                    for part in (ffn_hi, ffn_lo):
                        cols = part[:, :].rearrange("p (j h n) -> p j h n", h=2, n=P)[:, :, h, :]
                        last = nc.tensor.matmul(sum_bank(c)[:, 0:2 * P], merge16[:, h, :], cols,
                                                start=(h == 0 and part is ffn_hi), stop=(h == 1 and part is ffn_lo))
                last.then_inc(fin_done, 1)

            def chunk(c):
                tokens = xp[:, bass.ds(c, 1), :].rearrange("p o n -> p (o n)")
                weights = dt[:, bass.ds(c, 1), :].rearrange("p o n -> p (o n)")
                for e in range(E):
                    n = E * c + e
                    wait_past(pe, silu_done, n - 1)
                    nc.tensor.matmul(bank[e % 2][:, :], w1_hi[:, e, :], tokens, start=True, stop=False)
                    nc.tensor.matmul(bank[e % 2][:, :], w1_lo[:, e, :], tokens, start=False, stop=True).then_inc(h1_done, 1)
                    wait_past(pe, both_done, n - 1)
                    nc.tensor.matmul(bank[2 + e % 2][:, :], w2_hi[:, e, :], tokens, start=True, stop=False)
                    nc.tensor.matmul(bank[2 + e % 2][:, :], w2_lo[:, e, :], tokens, start=False, stop=True).then_inc(h2_done, 1)
                    if ce := before(c, e, DOWN_LAG):
                        down(*ce, step=n)
                    else:
                        wait_past(pe, hid_done, n - 1)
                    nc.tensor.matmul(bank[4 + e % 2][:, :], sel[:, e, :], weights, start=True, stop=True).then_inc(bcast_done, 1)
                    if e == FIN_AT and not first_chunk(c):
                        merge_parts(c - 1)

            over_chunks(pe, chunk)
            for e in range(E - DOWN_LAG, E):
                down(CHUNKS - 1, e)
            merge_parts(CHUNKS - 1)

        @block.vector
        def _(dve):
            own = [0]

            def step(ins):
                own[0] += 1
                ins.then_inc(dve_own, 1)
                dve.wait_ge(dve_own, own[0])

            nc.vector.memset(w_in_bd[:, :], 0.0)
            nc.vector.memset(w_out_bd[:, :], 0.0).then_inc(zeroed, 1)
            nc.vector.memset(eps_conv[:, :], EPS_CONV_LN).then_inc(eps_set, 1)
            nc.vector.memset(eps_ffn[:, :], EPS_FFN_LN).then_inc(eps_set, 1)
            nc.vector.memset(res[:, :], 0.0).then_inc(res_done, 1)
            dve.wait_ge(in_cst, 16)
            nc.vector.tensor_copy(ident16[:, :], ident)
            nc.vector.tensor_copy(merge16[:, :, :], merge)
            nc.vector.tensor_copy(identb[:, :], ident).then_inc(id16_set, 1)
            dve.wait_ge(in_bw, 16)
            nc.vector.tensor_copy(bw_cols[:, :, :], bw_rows[:, :].unsqueeze(1).to_broadcast([AR, B, M])).then_inc(bw_set, 1)

            for n in range(NBLK):
                dve.wait_ge(std_done, n + 1)
                nc.vector.reciprocal(rstd[:, n % 2, :], std[:, n % 2, :]).then_inc(rstd_done, 1)
                dve.wait_ge(rstd_done, n + 1)
                nc.vector.tensor_tensor(ln_q[:, n, :, :].rearrange("p q (x y) -> p q x y", y=16), by_quadrants(bank[n % 4][:, :]),
                                        by_quadrants(rstd[:, n % 2, :]), ALU.mult).then_inc(ln_done, 1)

            def butterfly(out_tile, upper, lower):
                up, low = (t.rearrange("p (q n) -> p q n", q=2) for t in (upper, lower))
                nc.vector.tensor_tensor(fold1[:, 0, :, :], up, low, ALU.add)
                step(nc.vector.tensor_tensor(fold1[:, 1, :, :], up, low, ALU.subtract))
                pairs = out_tile.rearrange("p (a b) n -> p a b n", a=2)
                nc.vector.tensor_tensor(pairs[:, :, 0, :], fold1[:, :, 0, :], fold1[:, :, 1, :], ALU.add)
                return nc.vector.tensor_tensor(pairs[:, :, 1, :], fold1[:, :, 0, :], fold1[:, :, 1, :], ALU.subtract)

            dve.wait_ge(proj_done, NBLK)
            dve.wait_ge(lower_out, 1)
            butterfly(fold2[:, :, :], bank[4][:, :], half_b[:, :]).then_inc(fold_done, 1)

            for k in range(2):
                dve.wait_ge(pow_a, k + 1)
                step(nc.vector.tensor_tensor(pw[:, k, :], power[:, k, 0, :], power[:, k, 1, :], ALU.add))
                nc.vector.tensor_scalar(pwc[:, k, :], pw[:, k, :], 2 * SQRT_MIN, None, ALU.max).then_inc(pow_sum, 1)
            dve.wait_ge(gain_done, 1)
            for k in range(2):
                dve.wait_ge(mag_done, k + 1)
                step(nc.vector.reciprocal(rmag[:, k, :], mag[:, k, :]))
                step(nc.vector.tensor_tensor(unit[:, k, :], bank[k][:, :], rmag[:, k, :], ALU.mult))
                step(nc.vector.scalar_tensor_tensor(unit1[:, k, :], pw[:, k, :], 0.0, unit[:, k, :], ALU.is_equal, ALU.add))
                step(nc.vector.scalar_tensor_tensor(zed[:, k, :], unit1[:, k, :], EPS_MAG, bank[k][:, :], ALU.mult, ALU.add))
                nc.vector.tensor_tensor(filt[:, 2 * k:2 * k + 2, :].rearrange("p c n -> p (c n)"), zed[:, k, :], bank[6 + k][:, :],
                                        ALU.mult).then_inc(filt_done, 1)
            dve.wait_ge(inv_done, 2)
            dve.wait_ge(odd_out, 1)
            butterfly(enh[:, :, :], bank[0][:, :], half_b[:, :]).then_inc(enh_done, 1)

            for qx in range(2):
                for g in range(G):
                    idx = qx * G + g
                    dve.wait_ge(outp_done, idx + 1)
                    dve.wait_ge(xy_done, 2 * g + qx + 1)
                    dst = xs_v[:, g, 16 * qx:16 * qx + 16, :].rearrange("p x (q y) -> p q x y", q=2)
                    src = bank[(2 + idx) % 8][:, :].rearrange("p (q x y) -> p q x y", q=2, x=16)
                    nc.vector.tensor_tensor(dst, src, dst, ALU.add).then_inc(x1_done, 1)

            for n in range(NBLK):
                dve.wait_ge(censq_done, n + 1)
                nc.vector.tensor_copy(cen[:, 8 * n:8 * n + 8, :].rearrange("p t c -> p (t c)"), bank[n % 4][:, :]).then_inc(cen_done, 1)
                nc.vector.tensor_reduce(ssq[:, 8 * n:8 * n + 8], cen_sq[:, n % 2, :].rearrange("p (t c) -> p t c", t=8),
                                        AX_X, ALU.add).then_inc(ssq_done, 1)
            dve.wait_ge(stdt_done, 1)
            nc.vector.reciprocal(rstd_t[:, :], std_t[:, :]).then_inc(rstdt_done, 1)
            dve.wait_ge(rstdt_done, 1)

            def low_part(c):
                dve.wait_ge(hi_done, c + 1)
                if c >= 2:
                    dve.wait_ge(xp_ps, c - 1)
                nc.vector.tensor_tensor(parts[:, c % 2, :, 1, :], tok[:, c % 2, :, :], parts[:, c % 2, :, 0, :],
                                        ALU.subtract).then_inc(lo_done, 1)

            for c in range(CHUNKS):
                if c >= 2:
                    dve.wait_ge(lo_done, c - 1)
                nc.vector.tensor_tensor(tok[:, c % 2, :, :], cen[:, SUB * c:SUB * (c + 1), :],
                                        rstd_t[:, SUB * c:SUB * (c + 1)].unsqueeze(2).to_broadcast([P, SUB, C]),
                                        ALU.mult).then_inc(tok_done, 1)
                if c >= 1:
                    low_part(c - 1)
            low_part(CHUNKS - 1)

            dve.wait_ge(lg_done, CHUNKS)
            dve.wait_ge(in_gate, 16 * 3)
            half = TILES // 2
            for k in range(2):
                last = nc.vector.scalar_tensor_tensor(lg[:, k * half:(k + 1) * half, :],
                                                      bank[4 + k][:, :].rearrange("p (t e) -> p t e", e=E), 1.0 / WSCALE,
                                                      gate_b_all[:, :].unsqueeze(1).to_broadcast([P, half, E]), ALU.mult, ALU.add)
            step(last)

            def over_experts(t):
                return t.unsqueeze(2).to_broadcast([P, TILES, E])

            def first_of_largest(onehot, logit, largest):
                step(nc.vector.tensor_reduce(largest[:, :], logit[:, :, :], AX_X, ALU.max))
                step(nc.vector.tensor_tensor(cand[:, :, :], logit[:, :, :], over_experts(largest[:, :]), ALU.is_equal))
                step(nc.vector.tensor_tensor(cand[:, :, :], cand[:, :, :], rev_iota.unsqueeze(1).to_broadcast([P, TILES, E]), ALU.mult))
                step(nc.vector.tensor_reduce(top[:, :], cand[:, :, :], AX_X, ALU.max))
                step(nc.vector.tensor_tensor(onehot[:, :, :], cand[:, :, :], over_experts(top[:, :]), ALU.is_equal))

            first_of_largest(first, lg, m1)
            step(nc.vector.scalar_tensor_tensor(lg2[:, :, :], first[:, :, :], -FAR, lg[:, :, :], ALU.mult, ALU.add))
            first_of_largest(second, lg2, m2)
            nc.vector.tensor_tensor(gap[:, :], m2[:, :], m1[:, :], ALU.subtract).then_inc(gap_done, 1)
            dve.wait_ge(ratio_done, 1)
            step(nc.vector.tensor_scalar(wt2[:, :], ratio[:, :], 1.0, WSCALE / HSCALE, ALU.add, ALU.mult))
            step(nc.vector.reciprocal(wt1[:, :], wt2[:, :]))
            step(nc.vector.tensor_tensor(wt2[:, :], wt1[:, :], ratio[:, :], ALU.mult))
            step(nc.vector.tensor_tensor(first[:, :, :], first[:, :, :], over_experts(wt1[:, :]), ALU.mult))
            step(nc.vector.tensor_tensor(second[:, :, :], second[:, :, :], over_experts(wt2[:, :]), ALU.mult))
            step(nc.vector.tensor_tensor(disp[:, :, :], first[:, :, :], second[:, :, :], ALU.add))
            step(nc.vector.tensor_copy(disp_parts[:, :, 0, :], disp[:, :, :]))
            step(nc.vector.tensor_tensor(rest[:, :, :], disp[:, :, :], disp_parts[:, :, 0, :], ALU.subtract))
            step(nc.vector.tensor_copy(disp_parts[:, :, 1, :], rest[:, :, :]))
            nc.vector.tensor_tensor(disp_parts[:, :, 2, :], rest[:, :, :], disp_parts[:, :, 1, :], ALU.subtract).then_inc(disp_done, 1)
            for n in range(CHUNKS // 2):
                dve.wait_ge(dt_ps, n + 1)
                nc.vector.tensor_copy(dt[:, 2 * n:2 * n + 2, :].rearrange("p c n -> p (c n)"),
                                      bank[2 + n % 2][0:DPARTS * E, :].bitcast(BF16)).then_inc(dt_done, 1)

            def weigh(c, e):
                n = E * c + e
                dve.wait_ge(bcast_done, n + 1)
                dve.wait_ge(both_done, n + 1)
                wait_past(dve, hidlo_done, n - SLOTS + 1)
                nc.vector.tensor_tensor(hid[:, e % SLOTS, :], bank[4 + e % 2][:, :], both[e % SLOTS], ALU.mult).then_inc(hid_done, 1)

            def sum_low_part(c):
                dve.wait_ge(ffnhi_done, c + 1)
                nc.vector.scalar_tensor_tensor(ffn_lo[:, :], sum_bank(c), 1.0 / (WSCALE * HSCALE), ffn_hi[:, :],
                                               ALU.mult, ALU.subtract).then_inc(ffn_done, 1)

            def result(c):
                dve.wait_ge(fin_done, c + 1)
                wait_past(dve, stored, 16 * c)
                nc.vector.tensor_tensor(res[:, :], sum_bank(c)[:, 0:2 * P], xs[:, bass.ds(2 * P * c, 2 * P)], ALU.add).then_inc(res_done, 1)

            def chunk(c):
                for e in range(E):
                    n = E * c + e
                    if ce := before(c, e, 1):
                        weigh(*ce)
                    dve.wait_ge(silu_done, n + 1)
                    dve.wait_ge(h2_done, n + 1)
                    wait_past(dve, hid_done, n - SLOTS + 1)
                    nc.vector.tensor_tensor(both[e % SLOTS], bank[2 + e % 2][:, :], gated[:, e % 2, :], ALU.mult).then_inc(both_done, 1)
                    if e == DOWN_LAG + 1 and not first_chunk(c):
                        sum_low_part(c - 1)
                    if e == FIN_AT + 1 and not first_chunk(c):
                        result(c - 1)

            over_chunks(dve, chunk)
            weigh(CHUNKS - 1, E - 1)
            sum_low_part(CHUNKS - 1)
            result(CHUNKS - 1)

        @block.gpsimd
        def _(pool):
            pool.wait_ge(in_gate, 16 * 3)
            nc.gpsimd.tensor_scalar(gate_raw[:, :], gate_raw[:, :], WSCALE, None, ALU.mult).then_inc(pool_own, 1)
            pool.wait_ge(pool_own, 1)
            nc.gpsimd.tensor_copy(gate_hi[:, :], gate_raw[:, :]).then_inc(pool_own, 1)
            pool.wait_ge(pool_own, 2)
            nc.gpsimd.tensor_tensor(gate_lo[:, :], gate_raw[:, :], gate_hi[:, :], ALU.subtract).then_inc(gate_set, 1)
            for n in range(NBLK):
                pool.wait_ge(ln_done, n + 1)
                cols = slice(n * BLK, (n + 1) * BLK)
                nc.gpsimd.tensor_tensor(by_quadrants(xs[:, cols]), by_quadrants(xs[:, cols]),
                                        ln_q[:, n, :, :].rearrange("p q (x y) -> p q x y", y=16), ALU.add).then_inc(xy_done, 1)
            for n, (raw, hi, lo, loaded) in enumerate((
                    (w1_raw[:, :, :], w1_hi[:, :, :], w1_lo[:, :, :], 2), (w2_raw[:, :, :], w2_hi[:, :, :], w2_lo[:, :, :], 2),
                    (w3_raw[:, :, :], w3_parts[:, :, 0, :], w3_parts[:, :, 1, :], 1))):
                pool.wait_ge((in_w1, in_w2, in_w3)[n], 16 * loaded)
                nc.gpsimd.tensor_scalar(raw, raw, WSCALE, None, ALU.mult).then_inc(pool_own, 1)
                pool.wait_ge(pool_own, 3 + 2 * n)
                nc.gpsimd.tensor_copy(hi, raw).then_inc(pool_own, 1)
                pool.wait_ge(pool_own, 4 + 2 * n)
                nc.gpsimd.tensor_tensor(lo, raw, hi, ALU.subtract).then_inc(wsplit, 1)
            pool.wait_ge(in_sel, 16)
            nc.gpsimd.tensor_copy(sel[:, :, :], sel_raw).then_inc(sel_set, 1)

            def low_part(c, e):
                n = E * c + e
                pool.wait_ge(hidhi_done, n + 1)
                wait_past(pool, down_done, n - SLOTS + 1)
                nc.gpsimd.tensor_tensor(hid_lo[:, e % SLOTS, :], hid[:, e % SLOTS, :], hid_hi[:, e % SLOTS, :],
                                        ALU.subtract).then_inc(hidlo_done, 1)

            def chunk(c):
                for e in range(E):
                    low_part(c, e)

            over_chunks(pool, chunk)


_INS = ["x", "L0_conv_w_in", "L0_conv_w_out", "L0_conv_bin_weights", "L0_ffn_gate_w", "L0_ffn_gate_b",
        "L0_ffn_w1", "L0_ffn_w2", "L0_ffn_w3"]


def kernel(**inputs):
    import concourse.bacc as bacc
    from concourse.bass_utils import run_bass_kernel_spmd

    nc = bacc.Bacc("TRN2", target_bir_lowering=False, num_devices=1)
    fwd, neg, inv = hartley_tables()
    tables = {"t_const": constant_tile(), "t_fwd": fwd, "t_neg": neg, "t_inv": inv, "t_bins": bin_table(), "t_sel": selector_table()}
    laid_out = {n: np.asarray(inputs[n]) for n in _INS}
    laid_out["L0_conv_w_in"] = laid_out["L0_conv_w_in"].T
    laid_out["L0_conv_w_out"] = laid_out["L0_conv_w_out"].T
    laid_out["L0_conv_bin_weights"] = laid_out["L0_conv_bin_weights"].reshape(M, AR).T
    for n in ("L0_ffn_w1", "L0_ffn_w2", "L0_ffn_w3"):
        laid_out[n] = laid_out[n].transpose(1, 0, 2)
    arrays, args = {}, []
    for name, a in list(laid_out.items()) + list(tables.items()):
        a = np.ascontiguousarray(a)
        arrays[f"in_{name}"] = a
        args.append(nc.dram_tensor(f"in_{name}", a.shape, mybir.dt.from_np(a.dtype), kind="ExternalInput").ap())
    args.append(nc.dram_tensor("out", (B, C, H, W), F32, kind="ExternalOutput").ap())
    build(nc, *args)
    r = run_bass_kernel_spmd(nc, [arrays], core_ids=[0])
    return r.results[0]["out"]
```

```python
from contextlib import ExitStack

import numpy as np

import concourse.bass as bass
from concourse import mybir

F32 = mybir.dt.float32
F16 = mybir.dt.float16
BF16 = mybir.dt.bfloat16
ALU = mybir.AluOpType
ACT = mybir.ActivationFunctionType
AX_X = mybir.AxisListType.X

B, C, H, W = 8, 64, 32, 32
M = 16
N_ANGLES, RADIUS_WIDTH, OVERLAP = 8, 8, 1.5
N_RADII = max(H // 2, W // 2) // RADIUS_WIDTH + 1
AR = N_ANGLES * N_RADII
E, HID = 16, 128
P = 128
G = B // 2
PIX = H * W
COLS = G * PIX
BLK = 512
NBLK = COLS // BLK
QUADS, KT, QPIX = 4, 2, PIX // 4
CHUNKS = 16
TOK = COLS * 2 // CHUNKS
SUB = TOK // P
TILES = CHUNKS * SUB
HT = TILES // 2
BT = TILES // NBLK
PTILES = TILES // 2
TOKW = P + 2 * M + 2
EPS_CONV_LN, EPS_FFN_LN, EPS_MAG = 1e-6, 1e-5, 1e-8
SQRT_MIN = 2.0 ** -116
WSCALE = 64.0
HSCALE = 8.0
FAR = 1e30
MEANS_AT = 4
DPARTS = 3
DROWS = DPARTS * 2 * E
WEIGH_LAG, LO_LAG, DOWN_LAG = 1, 2, 5
SLOTS, PSLOTS = 4, 8
BY_DMA = tuple(range(0, E - WEIGH_LAG, 2))
BY_PE = tuple(e for e in range(E) if e not in BY_DMA)
WROWS = len(BY_DMA)
WSPLIT = (WROWS + 1) // 2


ROWS_AT = DOWN_LAG
SUM_AT = DOWN_LAG - 1
FIN_AT = DOWN_LAG + 4


def first_chunk(c):
    return isinstance(c, int) and c == 0


def wait_past(eng, semaphore, value):
    if not isinstance(value, int) or value > 0:
        eng.wait_ge(semaphore, value)


def over_chunks(eng, chunk):
    chunk(0)
    with eng.Fori(1, CHUNKS) as c:
        chunk(c)


def before(c, e, lag):
    if e >= lag:
        return c, e - lag
    return None if first_chunk(c) else (c - 1, e - lag + E)


def hartley_tables():
    xy = np.arange(QPIX)
    x, y = xy // 16, xy % 16
    out = []
    for sign in (1.0, -1.0):
        t = np.empty((QPIX, 4, QPIX))
        for cls in range(4):
            u, v = 2 * x + cls // 2, 2 * y + cls % 2
            th = 2 * np.pi * ((np.outer(x, u) + np.outer(y, v)) % 32) / 32
            t[:, cls] = (np.cos(th) + sign * np.sin(th)) / 32
        out.append(t)
    fwd, neg = out
    inv = fwd.transpose(2, 1, 0)
    tile = lambda t: np.ascontiguousarray(t.reshape(KT, P, 4, QPIX).transpose(1, 0, 2, 3).reshape(P, -1).astype(np.float32))
    return tile(fwd), tile(neg), tile(inv)


def bin_table():
    f = np.float32
    y = np.arange(H, dtype=f)[:, None] - f(H // 2)
    x = np.arange(W, dtype=f)[None, :] - f(W // 2)
    r = np.sqrt(y * y + x * x)
    theta = (np.arctan2(y, x) + f(np.pi)) % f(np.pi)
    ridx = np.clip(np.floor(r / f(RADIUS_WIDTH)).astype(np.int32), 0, N_RADII - 1)
    delta = np.pi / N_ANGLES
    half = OVERLAP * delta / 2.0
    centers = (np.arange(N_ANGLES, dtype=f) * f(delta) + f(delta / 2.0))[:, None, None]
    dist = np.abs(theta[None] - centers)
    w = np.clip(f(1.0) - dist / f(half), f(0.0), None) * (dist < f(half))
    w = w / (w.sum(axis=0, keepdims=True) + f(1e-8))
    full = w[:, None] * (ridx[None, None] == np.arange(N_RADII)[None, :, None, None])
    full = np.fft.ifftshift(full.astype(np.float64), axes=(-2, -1))
    flip = np.roll(full[:, :, ::-1, ::-1], 1, axis=(-2, -1))
    sym = (full + flip) / 2
    a = np.arange(QPIX)
    cols = [sym[:, :, 2 * (a // 16) + cls // 2, 2 * (a % 16) + cls % 2] for cls in range(4)]
    return np.ascontiguousarray(np.stack(cols, 2).reshape(AR, PIX).astype(f))


def constant_tile():
    eye = np.eye(P)
    mean = np.kron(np.eye(2), np.full((C, C), 1.0 / C))
    rev = np.broadcast_to((E - np.arange(E))[None, :, None], (P, E, HT)).reshape(P, -1)
    merge = np.zeros((2, C, 2, 2, C))
    for h in range(2):
        merge[:, np.arange(C), h, h, np.arange(C)] = 1
    return np.ascontiguousarray(np.concatenate([eye, eye - mean, mean, merge.reshape(P, 2 * P), rev], 1).astype(np.float32))


def selector_table():
    sel = np.tile(np.eye(E), (DPARTS * 2, 1))[:, :, None]
    return np.ascontiguousarray(np.broadcast_to(sel, (DROWS, E, P)).reshape(DROWS, -1).astype(np.float32))


def build(nc, x, w_in, w_out, bin_w, gate_w, gate_b, w1, w2, w3, t_const, t_fwd, t_neg, t_inv, t_bins, t_sel, out):
    ctx = ExitStack()
    with ctx:
        def sb(name, shape, dt=F32):
            return ctx.enter_context(nc.sbuf_tensor(name, shape, dt))

        def sem(name):
            return ctx.enter_context(nc.semaphore(name))

        cst = sb("cst", [P, 5 * P])
        ident, centre, mean64 = cst[:, 0:P], cst[:, P:2 * P], cst[:, 2 * P:3 * P]
        merge = cst[:, 3 * P:5 * P].rearrange("p (h m) -> p h m", h=2)
        rev_raw = sb("rev_raw", [P, E * HT])
        rev_iota = sb("rev_iota", [P, E, HT], BF16)
        ident16 = sb("ident16", [P, P], F16)
        merge16 = sb("merge16", [P, 2, P], F16)
        identb = sb("identb", [P, P], BF16)
        warm = sb("warm", [P, 1])
        eps_conv, eps_ffn = sb("eps_conv", [P, 1]), sb("eps_ffn", [P, 1])
        w_in_bd = sb("w_in_bd", [P, 2 * M])
        w_out_bd = sb("w_out_bd", [P, 2 * M])
        w_out_all = sb("w_out_all", [P, P])
        w_outs = sb("w_outs", [P, P])
        w_mean = sb("w_mean", [P, G, 2])
        cw = sb("cw", [P, TOKW])
        bw_rows = sb("bw_rows", [AR, M])
        bw_cols = sb("bw_cols", [AR, B, M])
        shared = sb("shared", [P, 8, PIX])
        fwd, neg, inv = (shared[:, 2 * n:2 * n + 2, :].rearrange("p k (c n) -> p k c n", c=4) for n in range(3))
        bins = shared[0:AR, 6, :]
        filt_t = shared[:, 7, :].rearrange("p (c k n) -> p c k n", c=4, k=KT)
        xp = shared[:, 0:4, :].rearrange("p a n -> p (a n)").bitcast(F16).rearrange("p (c n) -> p c n", c=CHUNKS)
        dt = shared[0:DROWS, 4:8, :].rearrange("p a n -> p (a n)").bitcast(BF16).rearrange("p (c n) -> p c n", c=CHUNKS)
        gate_raw = sb("gate_raw", [P, E])
        gate_hi, gate_lo = sb("gate_hi", [P, E], F16), sb("gate_lo", [P, E], F16)
        gate_b_all = sb("gate_b_all", [P, E])
        w1_raw = sb("w1_raw", [P, E, HID])
        w23_raw = sb("w23_raw", [P, E * (HID + C)])
        w2_raw = w23_raw[:, 0:E * HID].rearrange("p (e n) -> p e n", e=E)
        w3_raw = w23_raw[:, E * HID:].rearrange("p (e n) -> p e n", e=E)
        w1_hi, w2_hi = sb("w1_hi", [P, E, HID], F16), sb("w2_hi", [P, E, HID], F16)
        w1_lo, w2_lo = sb("w1_lo", [P, E, HID], F16), sb("w2_lo", [P, E, HID], F16)
        w3_parts = sb("w3_parts", [P, E, 2, C], F16)
        sel_raw = w1_raw[0:DROWS, :, :]
        sel = sb("sel", [DROWS, E, P], BF16)
        xs = sb("xs", [P, COLS])
        scratch = sb("scratch", [P, 4, 2, BLK])
        xq = scratch[:, :, :, :].rearrange("p a b n -> p (a b n)")
        ct = sb("ct", [P, PTILES, TOKW])
        ssq1, std1, rstd1, rstd1_1 = (sb(n, [P, TILES]) for n in ("ssq1", "std1", "rstd1", "rstd1_1"))
        half_b = sb("half_b", [P, BLK])
        fold1 = sb("fold1", [P, 2, 2, QPIX])
        fold2 = sb("fold2", [P, 4, QPIX])
        power = sb("power", [P, 2, 2, BLK])
        pw = sb("pw", [P, 2, BLK])
        proj = pw[:, :, :].rearrange("p a (u r) -> p (a u) r", r=2 * M)
        pwc = sb("pwc", [P, 2, BLK])
        mag = sb("mag", [P, 2, BLK])
        rmag, passed, guard, small = (scratch[:, k, :, :] for k in range(4))
        gain = sb("gain", [P, 2, BLK])
        filt = sb("filt", [P, 4, QPIX])
        enh = sb("enh", [P, 4, QPIX])
        cen_sq = sb("cen_sq", [P, 2, BLK])
        ssq = sb("ssq", [P, TILES])
        mean1 = sb("mean1", [P, TILES])
        std_t, rstd_t = sb("std_t", [P, TILES]), sb("rstd_t", [P, TILES])
        tok = sb("tok", [P, 2, BT, C])
        parts = sb("parts", [P, 2, BT, 2, C], F16)
        lg, lg2 = (t.rearrange("p k (e t) -> p k e t", e=E) for t in (mag[:, :, :], rmag))
        cand = sb("cand", [P, 2, E, HT], BF16)
        chosen = sb("chosen", [P, 2, 2, E, HT], BF16)
        m1, m2 = sb("m1", [P, 2, HT]), sb("m2", [P, 2, HT])
        top = sb("top", [P, 2, HT], BF16)
        gap, ratio, total = (sb(n, [P, 2, HT]) for n in ("gap", "ratio", "total"))
        wt = sb("wt", [P, 2, 2, HT])
        wt_parts = sb("wt_parts", [P, 2, DPARTS, 2, HT], BF16)
        disp_parts = w23_raw[:, :].bitcast(BF16).rearrange("p (k a b e t) -> p k a b e t", k=2, a=DPARTS, b=2, e=E)
        gated = fold1[:, :, :, :].rearrange("p a b n -> p a (b n)")
        both = [t[:, k, :] for t in (pw, pwc) for k in range(2)]
        hid = power[:, :, :, :].rearrange("p a b n -> p (a b) n")
        hid_hi, hid_lo = (ct[:, :, :].rearrange("p u n -> p (u n)")[:, k * PSLOTS * BLK // 2:(k + 1) * PSLOTS * BLK // 2]
                          .bitcast(F16).rearrange("p (k n) -> p k n", k=PSLOTS) for k in range(2))
        ffn = sb("ffn", [P, TOK])
        ffn_hi, ffn_lo = sb("ffn_hi", [P, TOK], F16), sb("ffn_lo", [P, TOK], F16)
        res = sb("res", [P, 2 * P])

        rows_dram = nc.dram_tensor("weight_rows", (CHUNKS, WROWS, TOK), F32).ap()
        row_slots = w1_raw[0:WROWS, :, :].rearrange("p e n -> p (e n)").rearrange("p (k n) -> p k n", n=TOK)
        wide = scratch[:, :, :, :].rearrange("p a b n -> p (a b) n")

        bank = [ctx.enter_context(nc.psum_tensor(f"bank{i}", [P, BLK], F32)) for i in range(6)]
        sums = ctx.enter_context(nc.psum_tensor("sums", [P, 2, BLK], F32))
        bank += [sums[:, k, :] for k in range(2)]

        def dt_bank(n):
            return bank[4 + n if n < CHUNKS // 4 else 6 + n % 2][0:DROWS, :].bitcast(BF16)

        def weights_bank(c, e):
            return e % 2 if first_chunk(c) or e >= E - WEIGH_LAG else (e // 2 + 1) % 2

        def weights_read(c, e):
            if first_chunk(c):
                return e - 1
            users = [f for f in BY_PE if weights_bank(c, f) == weights_bank(c, e)]
            earlier = [f for f in users if f < e]
            return E * c + (earlier[-1] if earlier else users[-1] - E) + 1

        def sum_bank(c):
            return bank[6 + c % 2] if isinstance(c, int) else sums[:, bass.ds(c % 2, 1), :].rearrange("p o n -> p (o n)")

        in_win, in_wout, in_bw, in_cst, in_gate = (sem(n) for n in ("in_win", "in_wout", "in_bw", "in_cst", "in_gate"))
        in_x = [sem(f"in_x{n}") for n in range(NBLK)]
        in_fwd, in_neg, in_inv, in_bins = sem("in_fwd"), sem("in_neg"), sem("in_inv"), sem("in_bins")
        in_w1, in_w2, in_w3 = sem("in_w1"), sem("in_w2"), sem("in_w3")
        zeroed, eps_set = sem("zeroed"), sem("eps_set")
        dve_own, pool_own = sem("dve_own"), sem("pool_own")
        id16_set, bw_set = sem("id16_set"), sem("bw_set")
        wraw_done, whi_done, wsplit = sem("wraw_done"), sem("whi_done"), sem("wsplit")
        gate_set = sem("gate_set")
        in_rev, rev_set, in_centre, centre_set, wide_set, w_ps, w_set = (sem(n) for n in ("in_rev", "rev_set", "in_centre", "centre_set", "wide_set", "w_ps", "w_set"))
        xq_done, ct_ps, sq_done, ct_done, ssq1_done, std1_done, rstd1_done, rstd1_1_done, base_done = (
            sem(n) for n in ("xq_done", "ct_ps", "sq_done", "ct_done", "ssq1_done", "std1_done", "rstd1_done",
                             "rstd1_1_done", "base_done"))
        fold_done, dft_done, gain_done, gain_out = (sem(n) for n in ("fold_done", "dft_done", "gain_done", "gain_out"))
        pow_a, pow_sum, ln_done, mag_done, filt_done, filt_tp, filt_to, inv_done = (
            sem(n) for n in ("pow_a", "pow_sum", "ln_done", "mag_done", "filt_done", "filt_tp", "filt_to", "inv_done"))
        even_out, enh_done, means_ps, mean1_done, x1t_done, x1_ps, x1_done = (sem(n) for n in ("even_out", "enh_done", "means_ps", "mean1_done", "x1t_done", "x1_ps", "x1_done"))
        cen_ps, cen_done, censq_done, ssq_done, stdt_done, rstdt_done = (
            sem(n) for n in ("cen_ps", "cen_done", "censq_done", "ssq_done", "stdt_done", "rstdt_done"))
        tok_done, hi_done, lo_done, xp_ps, xp_done = (sem(n) for n in ("tok_done", "hi_done", "lo_done", "xp_ps", "xp_done"))
        in_sel, sel_set, dt_ps, dt_act, dt_dve = (sem(n) for n in ("in_sel", "sel_set", "dt_ps", "dt_act", "dt_dve"))
        lg_done, lg_out, gap_done, ratio_done, disp_done = (sem(n) for n in ("lg_done", "lg_out", "gap_done", "ratio_done", "disp_done"))
        row_ps, row_out, wide_a, wide_b = (sem(n) for n in ("row_ps", "row_out", "wide_a", "wide_b"))
        row_stored = [sem(f"row_stored{k}") for k in range(SLOTS)]
        h1_done, h2_done, bcast_done, silu_done, both_done, hid_done, hidhi_done, hidlo_done = (
            sem(n) for n in ("h1_done", "h2_done", "bcast_done", "silu_done", "both_done", "hid_done", "hidhi_done",
                             "hidlo_done"))
        down_done, ffn_out, ffnhi_done, ffn_done, fin_done, res_done, stored = (
            sem(n) for n in ("down_done", "ffn_out", "ffnhi_done", "ffn_done", "fin_done", "res_done", "stored"))

        x_v = x.rearrange("(g h) c a b -> (h c) g (a b)", h=2)
        out_v = out.rearrange("(g h) c a b -> (h c) g (a b)", h=2)
        x_img = xs[:, :].rearrange("p (n k x q y) -> p n k q x y", n=NBLK, k=KT, q=2, y=16)
        ct_cen = ct[:, :, 0:P].rearrange("p u (h c) -> p u h c", h=2)

        weight_parts = ((w1_raw[:, :, :], w1_hi[:, :, :], w1_lo[:, :, :]), (w2_raw, w2_hi[:, :, :], w2_lo[:, :, :]),
                        (w3_raw, w3_parts[:, :, 0, :], w3_parts[:, :, 1, :]))

        def mean_cols(t):
            return t.rearrange("p (h c) -> p h c", h=2)[:, :, 0]

        def per_tile(t, width):
            return t.rearrange("p (u h) -> p u h", h=2).unsqueeze(3).to_broadcast([P, t.shape[-1] // 2, 2, width])

        block = ctx.enter_context(nc.Block())

        @block.sync
        def _(sp):
            sp.dma_start(cst[:, P:3 * P], t_const[:, P:3 * P]).then_inc(in_centre, 16)
            for n in range(NBLK):
                if n == 2:
                    sp.dma_start(cst[:, 0:P], t_const[:, 0:P]).then_inc(in_cst, 16)
                    sp.dma_start(cst[:, 3 * P:5 * P], t_const[:, 3 * P:5 * P]).then_inc(in_cst, 16)
                sp.dma_start(xs[:, n * BLK:(n + 1) * BLK], x_v[:, n // 2, (n % 2) * BLK:(n % 2 + 1) * BLK]).then_inc(in_x[n], 16)
            sp.dma_start(fwd, t_fwd.rearrange("p (k c n) -> p k c n", k=KT, c=4)).then_inc(in_fwd, 16)
            sp.dma_start(neg, t_neg.rearrange("p (k c n) -> p k c n", k=KT, c=4)).then_inc(in_neg, 16)
            sp.dma_start(bins, t_bins).then_inc(in_bins, 16)
            for n, (w, raw) in enumerate(((w1, w1_raw), (w2, w2_raw))):
                for h in range(2):
                    sp.dma_start(raw[h * C:(h + 1) * C, :, :], w).then_inc((in_w1, in_w2)[n], 16)
            sp.dma_start(inv, t_inv.rearrange("p (k c n) -> p k c n", k=KT, c=4)).then_inc(in_inv, 16)
            sp.dma_start(w3_raw, w3).then_inc(in_w3, 16)
            sp.dma_start(rev_raw[:, :], t_const[:, 5 * P:]).then_inc(in_rev, 16)
            for h in range(2):
                sp.dma_start(gate_raw[h * C:(h + 1) * C, :], gate_w).then_inc(in_gate, 16)
            sp.dma_start(gate_b_all[:, :], gate_b.rearrange("(o e) -> o e", o=1).to_broadcast([P, E])).then_inc(in_gate, 16)
            sp.wait_ge(wsplit, 1)
            sp.dma_start(sel_raw, t_sel.rearrange("p (e n) -> p e n", e=E)).then_inc(in_sel, 16)

            def store_row(c):
                sp.wait_ge(row_out, c)
                sp.dma_start(rows_dram[c, :, :], row_slots[:, c % SLOTS, :]).then_inc(row_stored[c % SLOTS], 16)

            def load_wide(c, h):
                half = slice(0, WSPLIT) if h == 0 else slice(WSPLIT, WROWS)
                src = rows_dram[bass.ds(c, 1), half, :].to_broadcast([P, half.stop - half.start, TOK])
                sp.dma_start(wide[:, half, :], src).then_inc((wide_a, wide_b)[h], 16)

            def store(c):
                sp.wait_ge(res_done, c + 2)
                g, q = c // (PIX // (2 * P)), c % (PIX // (2 * P))
                dst = out_v[:, bass.ds(g, 1), bass.ds(q * (2 * P), 2 * P)].rearrange("p o n -> p (o n)")
                sp.dma_start(dst, res[:, :]).then_inc(stored, 16)

            for c in range(1, CHUNKS // 2):
                store_row(c)
            sp.wait_ge(row_stored[1], 16)
            sp.wait_ge(disp_done, 2)
            for h in range(2):
                load_wide(1, h)
            for c in range(CHUNKS // 2, CHUNKS):
                store_row(c)
            for c in range(CHUNKS - SLOTS, CHUNKS):
                sp.wait_ge(row_stored[c % SLOTS], 16 * ((c - 1) // SLOTS + 1))
            with sp.Fori(1, CHUNKS - 1) as c:
                sp.wait_ge(hid_done, E * c + BY_DMA[WSPLIT - 1] + 1)
                load_wide(c + 1, 0)
                store(c - 1)
                sp.wait_ge(hid_done, E * c + BY_DMA[-1] + 1)
                load_wide(c + 1, 1)
            for c in range(CHUNKS - 2, CHUNKS):
                store(c)
            sp.wait_ge(stored, 16 * CHUNKS)

        @block.scalar
        def _(act):
            def load_table(func):
                nc.scalar.activation(warm[:, :], eps_conv[:, :], func)

            act.wait_ge(eps_set, 2)
            act.wait_ge(zeroed, 1)
            for h in range(2):
                act.dma_start(w_in_bd[h * C:(h + 1) * C, h * M:(h + 1) * M], w_in).then_inc(in_win, 16)
            load_table(ACT.Sqrt)

            def squares(n):
                if n >= 2:
                    act.wait_ge(ssq1_done, n - 1)
                for k in range(2):
                    act.wait_ge(ct_ps, 2 * n + k + 1)
                    nc.scalar.activation(cen_sq[:, n % 2, k * 2 * P:(k + 1) * 2 * P].rearrange("p (u n) -> p u n", u=2),
                                         bank[(2 * n + k) % 6][:, 0:2 * TOKW].rearrange("p (u n) -> p u n", u=2)[:, :, 0:P],
                                         ACT.Square).then_inc(sq_done, 1)

            for n in range(NBLK):
                act.wait_ge(in_x[n], 16)
                for k in range(KT):
                    last = nc.scalar.copy(xq[:, (2 * n + k) * 2 * P:(2 * n + k + 1) * 2 * P].rearrange("p (q x y) -> p q x y", q=2, y=16),
                                          x_img[:, n, k, :, :, :])
                last.then_inc(xq_done, 1)
                if n == 0:
                    act.wait_ge(w_ps, 1)
                    nc.scalar.copy(cw[:, P:P + 2 * M], bank[7][:, 0:2 * M]).then_inc(w_set, 1)
                else:
                    squares(n - 1)
            squares(NBLK - 1)
            act.wait_ge(ssq1_done, NBLK)
            nc.scalar.activation(std1[:, :], ssq1[:, :], ACT.Sqrt, bias=eps_conv[:, :], scale=1.0 / C).then_inc(std1_done, 1)
            act.wait_ge(w_ps, 2)
            nc.scalar.copy(w_outs[:, :], bank[7][:, 0:P])
            for g in range(G):
                rows = slice(2 * M * g, 2 * M * (g + 1))
                last = nc.scalar.copy(w_mean[rows, g, :], mean_cols(bank[7][rows, P:2 * P]))
            last.then_inc(w_set, 1)

            def high_weights(n):
                raw, hi, _ = weight_parts[n]
                act.wait_ge((in_w1, in_w2, in_w3)[n], (32, 32, 16)[n])
                nc.scalar.activation(raw, raw, ACT.Copy, scale=WSCALE).then_inc(wraw_done, 1)
                act.wait_ge(wraw_done, n + 1)
                nc.scalar.copy(hi, raw).then_inc(whi_done, 1)

            high_weights(0)
            load_table(ACT.Ln)
            high_weights(1)
            def powers(k):
                act.wait_ge(dft_done, k + 1)
                nc.scalar.activation(power[:, k, 0, :], bank[k][:, :], ACT.Square)
                nc.scalar.activation(power[:, k, 1, :], bank[2 + k][:, :], ACT.Square).then_inc(pow_a, 1)

            def log_power(k):
                act.wait_ge(pow_sum, k + 1)
                nc.scalar.activation(mag[:, k, :], pwc[:, k, :], ACT.Ln, scale=0.5).then_inc(ln_done, 1)

            def inverse_magnitude(k):
                act.wait_ge(ln_done, k + 1)
                nc.scalar.activation(rmag[:, k, :], mag[:, k, :], ACT.Exp, scale=-0.5).then_inc(mag_done, 1)

            for k in range(2):
                act.wait_ge(gain_done, k + 1)
                nc.scalar.copy(gain[:, k, :], bank[6 + k][:, :]).then_inc(gain_out, 1)
            powers(0)
            log_power(0)
            powers(1)
            inverse_magnitude(0)
            log_power(1)
            inverse_magnitude(1)
            for k in range(2):
                act.wait_ge(filt_tp, k + 1)
                nc.scalar.copy(filt_t[:, 2 * k:2 * k + 2, :, :], bank[4 + k][:, :].rearrange("p (c k n) -> p c k n", c=2, k=KT)).then_inc(filt_to, 1)
                if k == 0:
                    high_weights(2)
            load_table(ACT.Sqrt)
            act.wait_ge(inv_done, 1)
            nc.scalar.copy(half_b[:, :], bank[0][:, :]).then_inc(even_out, 1)
            act.wait_ge(in_sel, 16)
            nc.scalar.copy(sel[:, :, :], sel_raw).then_inc(sel_set, 1)

            def high(n):
                act.wait_ge(tok_done, n + 1)
                if n >= 2:
                    act.wait_ge(xp_ps, n - 1)
                nc.scalar.copy(parts[:, n % 2, :, 0, :], tok[:, n % 2, :, :]).then_inc(hi_done, 1)

            def transposed_out(n):
                act.wait_ge(xp_ps, n + 1)
                nc.scalar.copy(xp[:, 2 * n:2 * n + 2, :].rearrange("p c n -> p (c n)"),
                               bank[4 + n % 2][:, :].bitcast(F16)).then_inc(xp_done, 1)

            for n in range(NBLK + 3):
                if n < NBLK:
                    act.wait_ge(cen_done, n + 1)
                    if n >= 2:
                        act.wait_ge(ssq_done, n - 1)
                    nc.scalar.activation(cen_sq[:, n % 2, :].rearrange("p (u n) -> p u n", u=4), ct[:, 4 * n:4 * n + 4, 0:P],
                                         ACT.Square).then_inc(censq_done, 1)
                if 1 <= n <= NBLK:
                    cols = slice(BT * (n - 1), BT * n)
                    act.wait_ge(ssq_done, n)
                    nc.scalar.activation(std_t[:, cols], ssq[:, cols], ACT.Sqrt, bias=eps_ffn[:, :], scale=1.0 / C).then_inc(stdt_done, 1)
                if 2 <= n < NBLK + 2:
                    high(n - 2)
                if n >= 3:
                    transposed_out(n - 3)

            def x1_out(n):
                act.wait_ge(x1_ps, n + 1)
                nc.scalar.copy(xs[:, n * BLK:(n + 1) * BLK], bank[n % 4][:, :]).then_inc(x1_done, 1)

            def gap_exponential(k):
                act.wait_ge(gap_done, k + 1)
                nc.scalar.activation(ratio[:, k, :], gap[:, k, :], ACT.Exp).then_inc(ratio_done, 1)

            def weights_out(n):
                act.wait_ge(dt_ps, n + 1)
                nc.scalar.copy(dt[:, 2 * n:2 * n + 2, :].rearrange("p c n -> p (c n)"),
                               dt_bank(n)).then_inc(dt_act, 1)

            def row(c):
                act.wait_ge(row_ps, c)
                if c > SLOTS:
                    act.wait_ge(row_stored[c % SLOTS], 16 * ((c - 1) // SLOTS))
                src = bank[(c - 1) % 4] if c < CHUNKS // 2 else bank[7]
                nc.scalar.copy(row_slots[:, c % SLOTS, :], src[0:WROWS, :]).then_inc(row_out, 1)

            load_table(ACT.Exp)
            gap_exponential(0)
            for n in range(NBLK):
                x1_out(n)
            for n in range(CHUNKS // 4):
                if n == CHUNKS // 4 - 1:
                    gap_exponential(1)
                weights_out(n)
            for c in range(1, CHUNKS // 2):
                row(c)
            load_table(ACT.Silu)

            def high_part(c, e):
                n = E * c + e
                act.wait_ge(hid_done, n + 1)
                wait_past(act, down_done, n - PSLOTS + 1)
                nc.scalar.copy(hid_hi[:, e % PSLOTS, :], hid[:, e % SLOTS, :]).then_inc(hidhi_done, 1)

            def chunk_sum(c):
                act.wait_ge(down_done, E * (c + 1))
                wait_past(act, fin_done, c)
                nc.scalar.activation(ffn[:, :], sum_bank(c), ACT.Copy, scale=1.0 / (WSCALE * HSCALE)).then_inc(ffn_out, 1)
                act.wait_ge(ffn_out, c + 1)
                nc.scalar.copy(ffn_hi[:, :], ffn[:, :]).then_inc(ffnhi_done, 1)

            def chunk(c):
                for e in range(E):
                    n = E * c + e
                    act.wait_ge(h1_done, n + 1)
                    wait_past(act, both_done, n - 1)
                    nc.scalar.activation(gated[:, e % 2, :], bank[e % 2][:, :], ACT.Silu, scale=1.0 / WSCALE).then_inc(silu_done, 1)
                    if ce := before(c, e, LO_LAG):
                        high_part(*ce)
                    if first_chunk(c) and e in (1, 3):
                        weights_out(CHUNKS // 4 + e)
                    if first_chunk(c) and ROWS_AT <= e < ROWS_AT + CHUNKS // 2:
                        row(CHUNKS // 2 + e - ROWS_AT)
                    if e == DOWN_LAG and not first_chunk(c):
                        chunk_sum(c - 1)

            over_chunks(act, chunk)
            for e in range(E - LO_LAG, E):
                high_part(CHUNKS - 1, e)
            chunk_sum(CHUNKS - 1)

        @block.tensor
        def _(pe):
            def keep_warm(count, spare):
                for _ in range(count):
                    nc.tensor.matmul(spare[:, :], centre, xs[:, 0:BLK], start=True, stop=True)

            pe.wait_ge(in_centre, 16)
            pe.wait_ge(in_win, 16 * 2)
            nc.tensor.matmul(bank[7][:, 0:2 * M], centre, w_in_bd[:, :], start=True, stop=True).then_inc(w_ps, 1)
            pe.wait_ge(centre_set, 1)
            pe.wait_ge(w_set, 1)
            for m in range(PTILES // 2):
                pe.wait_ge(xq_done, m // 2 + 1)
                if m >= 6:
                    pe.wait_ge(ct_done, m - 5)
                for k in range(2):
                    col = (2 * m + k) * P
                    last = nc.tensor.matmul(bank[m % 6][:, k * TOKW:(k + 1) * TOKW], xq[:, col:col + P], cw[:, :], start=True, stop=True)
                last.then_inc(ct_ps, 1)

            pe.wait_ge(wide_set, 1)
            pe.wait_ge(w_set, 1)
            nc.tensor.matmul(bank[7][:, 0:2 * P], w_out_all[:, :], cst[:, P:3 * P], start=True, stop=True).then_inc(w_ps, 1)

            pe.wait_ge(bw_set, 1)
            pe.wait_ge(in_bins, 16)
            pe.wait_ge(w_set, 2)
            for k in range(2):
                last = nc.tensor.matmul(bank[6 + k][:, :], bw_cols[:, :, :].rearrange("a b m -> a (b m)"),
                                        bins[:, k * BLK:(k + 1) * BLK], start=True, stop=True)
                last.then_inc(gain_done, 1)

            pe.wait_ge(in_fwd, 16)
            pe.wait_ge(in_neg, 16)
            pe.wait_ge(fold_done, 1)
            for cls in range(4):
                for table, first_bank in ((fwd, 0), (neg, 2)):
                    dst = bank[first_bank + cls // 2][:, (cls % 2) * QPIX:(cls % 2 + 1) * QPIX]
                    for kt in range(KT):
                        last = nc.tensor.matmul(dst, fold2[:, cls, kt * P:(kt + 1) * P], table[:, kt, cls, :],
                                                start=(kt == 0), stop=(kt == KT - 1))
                if cls % 2:
                    last.then_inc(dft_done, 1)

            pe.wait_ge(in_cst, 16 * 2)
            pe.wait_ge(in_inv, 16)
            keep_warm(4, bank[4])
            for pu in range(2):
                pe.wait_ge(filt_done, pu + 1)
                for a in range(2 * KT):
                    cls, kt = 2 * pu + a // KT, a % KT
                    last = nc.tensor.transpose(bank[4 + pu][:, a * P:(a + 1) * P], filt[:, cls, kt * P:(kt + 1) * P], ident)
                last.then_inc(filt_tp, 1)
                if pu == 0:
                    keep_warm(1, bank[5])
                pe.wait_ge(filt_to, pu + 1)
                for pv in range(2):
                    for kt in range(KT):
                        last = nc.tensor.matmul(bank[pu][:, pv * QPIX:(pv + 1) * QPIX], filt_t[:, 2 * pu + pv, kt, :],
                                                inv[:, kt, 2 * pu + pv, :], start=(kt == 0), stop=(kt == KT - 1))
                last.then_inc(inv_done, 1)

            def project_back(n):
                g, qx = n // 2, n % 2
                rows = slice(2 * M * g, 2 * M * (g + 1))
                pe.wait_ge(enh_done, qx + 1)
                if n >= 3:
                    pe.wait_ge(cen_done, n - 2)
                for u in range(4):
                    kt, qy = u // 2, u % 2
                    last = nc.tensor.matmul(bank[n % 3][:, u * P:(u + 1) * P], enh[rows, 2 * qx + qy, kt * P:(kt + 1) * P],
                                            w_outs[rows, :], start=True, stop=True)
                last.then_inc(cen_ps, 1)

            def transpose_parts(n):
                pe.wait_ge(lo_done, n + 1)
                if n >= 2:
                    pe.wait_ge(xp_done, n - 1)
                for s in range(BT):
                    last = nc.tensor.transpose(bank[4 + n % 2][:, :].bitcast(F16)[:, s * P:(s + 1) * P],
                                               parts[:, n % 2, s, :, :].rearrange("p a c -> p (a c)"), ident16[:, :])
                last.then_inc(xp_ps, 1)

            def logits(n):
                pe.wait_ge(xp_done, n + 1)
                for t in range(BT * n, BT * (n + 1)):
                    c, s = t // SUB, t % SUB
                    dst = bank[6 + t * E // BLK][:, t * E % BLK:t * E % BLK + E]
                    lhs = xp[:, c, s * P:(s + 1) * P]
                    nc.tensor.matmul(dst, lhs, gate_hi[:, :], start=True, stop=False)
                    last = nc.tensor.matmul(dst, lhs, gate_lo[:, :], start=False, stop=True)
                last.then_inc(lg_done, 1)

            keep_warm(2, bank[3])
            for n in range(3):
                project_back(n)
            pe.wait_ge(id16_set, 1)
            pe.wait_ge(gate_set, 1)
            for n in range(NBLK):
                if n + 3 < NBLK:
                    project_back(n + 3)
                transpose_parts(n)
                if n >= 1:
                    logits(n - 1)
                if n == MEANS_AT:
                    for u in range(PIX // P):
                        qx, kt, qy = u // 4, u // 2 % 2, u % 2
                        last = nc.tensor.matmul(bank[3][:, u * B:(u + 1) * B], enh[:, 2 * qx + qy, kt * P:(kt + 1) * P],
                                         w_mean[:, :, :].rearrange("p g h -> p (g h)"), start=True, stop=True)
                    last.then_inc(means_ps, 1)
            logits(NBLK - 1)

            def transpose_weights(n):
                k, tile = 2 * n // (CHUNKS // 2), 2 * SUB * n % HT
                pe.wait_ge(disp_done, k + 1)
                for s in range(2 * SUB):
                    last = nc.tensor.transpose(dt_bank(n)[:, s * P:(s + 1) * P],
                                               disp_parts[:, k, :, :, :, tile + s].rearrange("p a b e -> p (a b e)"), identb[:, :])
                last.then_inc(dt_ps, 1)

            for n in range(NBLK):
                pe.wait_ge(x1t_done, n + 1)
                if n == 3:
                    pe.wait_ge(mean1_done, 1)
                if n >= 4:
                    pe.wait_ge(x1_done, n - 3)
                for u in range(4):
                    last = nc.tensor.transpose(bank[n % 4][:, u * P:(u + 1) * P], ct[:, 4 * n + u, 0:P], ident)
                last.then_inc(x1_ps, 1)
            def weight_row(c, dst):
                nc.tensor.matmul(dst[0:WROWS, :], sel[:, 0:BY_DMA[-1] + 1:2, 0], dt[:, c, :], start=True, stop=True).then_inc(row_ps, 1)

            for n in range(CHUNKS // 4):
                if n == 3:
                    pe.wait_ge(lg_out, 2)
                transpose_weights(n)
            pe.wait_ge(sel_set, 1)
            pe.wait_ge(x1_done, NBLK)
            pe.wait_ge(dt_act, CHUNKS // 4)
            for c in range(1, CHUNKS // 2):
                if c > 4:
                    pe.wait_ge(row_out, c - 4)
                weight_row(c, bank[(c - 1) % 4])
            pe.wait_ge(wsplit, 3)
            pe.wait_ge(row_out, CHUNKS // 2 - 1)

            def down(c, e):
                n = E * c + e
                if first_chunk(c) and e == 0:
                    pe.wait_ge(dt_dve, CHUNKS // 8)
                    pe.wait_ge(dt_act, CHUNKS // 4 + CHUNKS // 8)
                pe.wait_ge(hidhi_done, n + 1)
                if e == 0:
                    wait_past(pe, res_done, c)
                lhs = w3_parts[:, e, :, :].rearrange("p a c -> p (a c)")
                nc.tensor.matmul(sum_bank(c), lhs, hid_hi[:, e % PSLOTS, :], start=(e == 0), stop=False)
                pe.wait_ge(hidlo_done, n + 1)
                nc.tensor.matmul(sum_bank(c), lhs, hid_lo[:, e % PSLOTS, :], start=False, stop=(e == E - 1)).then_inc(down_done, 1)

            def merge_parts(c):
                pe.wait_ge(ffn_done, c + 1)
                for h in range(2):
                    for part in (ffn_hi, ffn_lo):
                        cols = part[:, :].rearrange("p (j h n) -> p j h n", h=2, n=P)[:, :, h, :]
                        last = nc.tensor.matmul(sum_bank(c)[:, 0:2 * P], merge16[:, h, :], cols,
                                                start=(h == 0 and part is ffn_hi), stop=(h == 1 and part is ffn_lo))
                last.then_inc(fin_done, 1)

            def chunk(c):
                tokens = xp[:, bass.ds(c, 1), :].rearrange("p o n -> p (o n)")
                weights = dt[:, bass.ds(c, 1), :].rearrange("p o n -> p (o n)")
                for e in range(E):
                    n = E * c + e
                    wait_past(pe, silu_done, n - 1)
                    nc.tensor.matmul(bank[e % 2][:, :], w1_hi[:, e, :], tokens, start=True, stop=False)
                    nc.tensor.matmul(bank[e % 2][:, :], w1_lo[:, e, :], tokens, start=False, stop=True).then_inc(h1_done, 1)
                    wait_past(pe, both_done, n - 1)
                    nc.tensor.matmul(bank[2 + e % 2][:, :], w2_hi[:, e, :], tokens, start=True, stop=False)
                    nc.tensor.matmul(bank[2 + e % 2][:, :], w2_lo[:, e, :], tokens, start=False, stop=True).then_inc(h2_done, 1)
                    by_dma = e in BY_DMA and not first_chunk(c)
                    if ce := before(c, e, DOWN_LAG):
                        down(*ce)
                    if not by_dma:
                        wait_past(pe, hid_done, weights_read(c, e))
                        nc.tensor.matmul(bank[4 + weights_bank(c, e)][:, :], sel[:, e, :], weights, start=True, stop=True).then_inc(bcast_done, 1)
                    if first_chunk(c) and e < CHUNKS // 4:
                        if e >= 2:
                            pe.wait_ge((dt_dve, dt_act)[e % 2], (1, CHUNKS // 4 + 1)[e % 2])
                        transpose_weights(CHUNKS // 4 + e)
                    if first_chunk(c) and ROWS_AT <= e < ROWS_AT + CHUNKS // 2:
                        other = CHUNKS // 2 + e - ROWS_AT
                        pe.wait_ge(row_out, other - 1)
                        weight_row(other, bank[7])
                    if e == FIN_AT and not first_chunk(c):
                        merge_parts(c - 1)

            over_chunks(pe, chunk)
            for e in range(E - DOWN_LAG, E):
                down(CHUNKS - 1, e)
            merge_parts(CHUNKS - 1)

        @block.vector
        def _(dve):
            own = [0]

            def step(ins):
                own[0] += 1
                ins.then_inc(dve_own, 1)
                dve.wait_ge(dve_own, own[0])

            nc.vector.memset(w_mean[:, :, :], 0.0)
            nc.vector.memset(w_in_bd[:, :], 0.0)
            nc.vector.memset(w_out_bd[:, :], 0.0).then_inc(zeroed, 1)
            nc.vector.memset(eps_conv[:, :], EPS_CONV_LN).then_inc(eps_set, 1)
            nc.vector.memset(eps_ffn[:, :], EPS_FFN_LN).then_inc(eps_set, 1)
            nc.vector.memset(res[:, :], 0.0).then_inc(res_done, 1)
            dve.wait_ge(in_centre, 16)
            nc.vector.tensor_copy(cw[:, 0:P], centre)
            nc.vector.tensor_copy(cw[:, P + 2 * M:TOKW], mean_cols(mean64)).then_inc(centre_set, 1)
            for m in range(PTILES // 2):
                dve.wait_ge(sq_done, m + 1)
                nc.vector.tensor_copy(ct[:, 2 * m:2 * m + 2, :].rearrange("p u n -> p (u n)"), bank[m % 6][:, 0:2 * TOKW]).then_inc(ct_done, 1)
                if m % 2:
                    n = m // 2
                    nc.vector.tensor_reduce(ssq1[:, BT * n:BT * (n + 1)], cen_sq[:, n % 2, :].rearrange("p (t c) -> p t c", c=C),
                                            AX_X, ALU.add).then_inc(ssq1_done, 1)
            dve.wait_ge(in_wout, 16 * 2)
            nc.vector.tensor_copy(w_out_all[:, :].rearrange("p (g m) -> p g m", g=G),
                                  w_out_bd[:, :].unsqueeze(1).to_broadcast([P, G, 2 * M])).then_inc(wide_set, 1)
            dve.wait_ge(in_bw, 16)
            nc.vector.tensor_copy(bw_cols[:, :, :], bw_rows[:, :].unsqueeze(1).to_broadcast([AR, B, M])).then_inc(bw_set, 1)
            dve.wait_ge(in_cst, 16 * 2)
            nc.vector.tensor_copy(ident16[:, :], ident)
            nc.vector.tensor_copy(merge16[:, :, :], merge)
            nc.vector.tensor_copy(identb[:, :], ident).then_inc(id16_set, 1)
            dve.wait_ge(std1_done, 1)
            nc.vector.reciprocal(rstd1[:, :], std1[:, :]).then_inc(rstd1_done, 1)
            dve.wait_ge(rstd1_done, 1)
            step(nc.vector.tensor_tensor(proj.rearrange("p u (h m) -> p u h m", h=2), ct[:, :, P:P + 2 * M].rearrange("p u (h m) -> p u h m", h=2),
                                         per_tile(rstd1[:, :], M), ALU.mult))

            def over_columns(out_tile):
                pairs = out_tile.rearrange("p (a b) n -> p a b n", a=2)
                nc.vector.tensor_tensor(pairs[:, :, 0, :], fold1[:, :, 0, :], fold1[:, :, 1, :], ALU.add)
                return nc.vector.tensor_tensor(pairs[:, :, 1, :], fold1[:, :, 0, :], fold1[:, :, 1, :], ALU.subtract)

            quads = proj.rearrange("p (g a k b) r -> p a b g k r", g=G, a=2, b=2)
            for sign, op in enumerate((ALU.add, ALU.subtract)):
                for qy in range(2):
                    last = nc.vector.tensor_tensor(fold1[:, sign, qy, :].rearrange("p (k g r) -> p g k r", k=KT, g=G),
                                                   quads[:, 0, qy, :, :, :], quads[:, 1, qy, :, :, :], op)
            step(last)
            over_columns(fold2[:, :, :]).then_inc(fold_done, 1)

            def power_sum(k):
                dve.wait_ge(pow_a, k + 1)
                step(nc.vector.tensor_tensor(pw[:, k, :], power[:, k, 0, :], power[:, k, 1, :], ALU.add))
                nc.vector.tensor_scalar(pwc[:, k, :], pw[:, k, :], 2 * SQRT_MIN, None, ALU.max).then_inc(pow_sum, 1)

            def pass_through(k):
                dve.wait_ge(gain_out, k + 1)
                nc.vector.tensor_tensor(passed[:, k, :], bank[k][:, :], gain[:, k, :], ALU.mult)
                step(nc.vector.scalar_tensor_tensor(guard[:, k, :], pw[:, k, :], 0.0, gain[:, k, :], ALU.is_equal, ALU.mult))
                step(nc.vector.scalar_tensor_tensor(guard[:, k, :], guard[:, k, :], EPS_MAG, passed[:, k, :], ALU.mult, ALU.add))

            def add_small(k):
                dve.wait_ge(mag_done, k + 1)
                step(nc.vector.scalar_tensor_tensor(small[:, k, :], passed[:, k, :], EPS_MAG, rmag[:, k, :], ALU.mult, ALU.mult))
                nc.vector.tensor_tensor(filt[:, 2 * k:2 * k + 2, :].rearrange("p c n -> p (c n)"), guard[:, k, :], small[:, k, :],
                                        ALU.add).then_inc(filt_done, 1)

            power_sum(0)
            pass_through(0)
            power_sum(1)
            add_small(0)
            pass_through(1)
            add_small(1)
            dve.wait_ge(in_rev, 16)
            nc.vector.tensor_copy(rev_iota[:, :, :].rearrange("p e t -> p (e t)"), rev_raw[:, :]).then_inc(rev_set, 1)
            dve.wait_ge(even_out, 1)
            dve.wait_ge(inv_done, 2)
            pairs = enh[:, :, :].rearrange("p (a b) n -> p a b n", a=2)
            even, odd = (t.rearrange("p (q n) -> p q n", q=2) for t in (half_b[:, :], bank[1][:, :]))
            for a, op in enumerate((ALU.add, ALU.subtract)):
                step(nc.vector.tensor_tensor(fold1[:, a, :, :], even, odd, op))
                nc.vector.tensor_tensor(pairs[:, a, 0, :], fold1[:, a, 0, :], fold1[:, a, 1, :], ALU.add)
                nc.vector.tensor_tensor(pairs[:, a, 1, :], fold1[:, a, 0, :], fold1[:, a, 1, :], ALU.subtract).then_inc(enh_done, 1)

            for n in range(NBLK + 2):
                if n < NBLK:
                    dve.wait_ge(cen_ps, n + 1)
                    dve.wait_ge(base_done, n + 1)
                    nc.vector.tensor_tensor(ct[:, 4 * n:4 * n + 4, 0:P], ct[:, 4 * n:4 * n + 4, 0:P],
                                            bank[n % 3][:, :].rearrange("p (u n) -> p u n", u=4), ALU.add).then_inc(cen_done, 1)
                if 1 <= n <= NBLK:
                    dve.wait_ge(censq_done, n)
                    nc.vector.tensor_reduce(ssq[:, BT * (n - 1):BT * n], cen_sq[:, (n - 1) % 2, :].rearrange("p (t c) -> p t c", c=C),
                                            AX_X, ALU.add).then_inc(ssq_done, 1)
                if n >= 2:
                    b = n - 2
                    dve.wait_ge(stdt_done, b + 1)
                    nc.vector.reciprocal(rstd_t[:, BT * b:BT * (b + 1)], std_t[:, BT * b:BT * (b + 1)]).then_inc(rstdt_done, 1)
                    dve.wait_ge(rstdt_done, b + 1)
                    if b >= 2:
                        dve.wait_ge(lo_done, b - 1)
                    nc.vector.tensor_tensor(tok[:, b % 2, :, :].rearrange("p (u h) c -> p u h c", h=2), ct_cen[:, 4 * b:4 * b + 4, :, :],
                                            per_tile(rstd_t[:, BT * b:BT * (b + 1)], C), ALU.mult).then_inc(tok_done, 1)

            dve.wait_ge(means_ps, 1)
            nc.vector.tensor_tensor(mean1[:, :].rearrange("p (g u h) -> p g u h", g=G, h=2),
                                    bank[3][:, 0:TILES].rearrange("p (u g h) -> p g u h", g=G, h=2),
                                    ct[:, :, P + 2 * M:TOKW].rearrange("p (g u) h -> p g u h", g=G), ALU.add).then_inc(mean1_done, 1)

            def route(k):
                def over_experts(t):
                    return t[:, k, :].unsqueeze(1).to_broadcast([P, E, HT])

                def largest_of(t, largest):
                    return nc.vector.tensor_reduce(largest[:, k, :], t[:, k, :, :].rearrange("p e t -> p t e"), AX_X, ALU.max)

                def first_of(onehot, logit, largest):
                    step(nc.vector.tensor_tensor(cand[:, k, :, :], logit[:, k, :, :], over_experts(largest), ALU.is_equal))
                    step(nc.vector.tensor_tensor(cand[:, k, :, :], cand[:, k, :, :], rev_iota[:, :, :], ALU.mult))
                    step(largest_of(cand, top))
                    step(nc.vector.tensor_tensor(onehot, cand[:, k, :, :], over_experts(top), ALU.is_equal))

                dve.wait_ge(lg_done, (k + 1) * NBLK // 2)
                nc.vector.scalar_tensor_tensor(lg[:, k, :, :], bank[6 + k][:, :].rearrange("p (t e) -> p e t", e=E), 1.0 / WSCALE,
                                               gate_b_all[:, :].unsqueeze(2).to_broadcast([P, E, HT]), ALU.mult, ALU.add).then_inc(lg_out, 1)
                dve.wait_ge(lg_out, k + 1)
                step(largest_of(lg, m1))
                first_of(chosen[:, k, 0, :, :], lg, m1)
                step(nc.vector.scalar_tensor_tensor(lg2[:, k, :, :], chosen[:, k, 0, :, :], -FAR, lg[:, k, :, :], ALU.mult, ALU.add))
                step(largest_of(lg2, m2))
                nc.vector.tensor_tensor(gap[:, k, :], m2[:, k, :], m1[:, k, :], ALU.subtract).then_inc(gap_done, 1)
                first_of(chosen[:, k, 1, :, :], lg2, m2)
                dve.wait_ge(ratio_done, k + 1)
                step(nc.vector.tensor_scalar(total[:, k, :], ratio[:, k, :], 1.0, WSCALE / HSCALE, ALU.add, ALU.mult))
                step(nc.vector.reciprocal(wt[:, k, 0, :], total[:, k, :]))
                step(nc.vector.tensor_tensor(wt[:, k, 1, :], wt[:, k, 0, :], ratio[:, k, :], ALU.mult))
                parts_of = [wt_parts[:, k, part, :, :] for part in range(DPARTS)]
                step(nc.vector.tensor_copy(parts_of[0], wt[:, k, :, :]))
                step(nc.vector.tensor_tensor(wt[:, k, :, :], wt[:, k, :, :], parts_of[0], ALU.subtract))
                step(nc.vector.tensor_copy(parts_of[1], wt[:, k, :, :]))
                step(nc.vector.tensor_tensor(parts_of[2], wt[:, k, :, :], parts_of[1], ALU.subtract))
                if k == 0:
                    dve.wait_ge(wsplit, 3)
                for choice in range(2):
                    for part in range(DPARTS):
                        last = nc.vector.tensor_tensor(disp_parts[:, k, part, choice, :, :], chosen[:, k, choice, :, :],
                                                       wt_parts[:, k, part, choice, :].unsqueeze(1).to_broadcast([P, E, HT]), ALU.mult)
                last.then_inc(disp_done, 1)

            def weights_out(n):
                dve.wait_ge(dt_ps, n + 1)
                nc.vector.tensor_copy(dt[:, 2 * n:2 * n + 2, :].rearrange("p c n -> p (c n)"),
                                      dt_bank(n)).then_inc(dt_dve, 1)

            route(0)
            route(1)
            def weigh(c, e):
                n = E * c + e
                if first_chunk(c) or e in BY_PE:
                    dve.wait_ge(bcast_done, n + 1 if first_chunk(c) else E + (c - 1) * len(BY_PE) + BY_PE.index(e) + 1)
                    weights = bank[4 + weights_bank(c, e)][:, :]
                else:
                    row = BY_DMA.index(e)
                    dve.wait_ge(wide_a if row < WSPLIT else wide_b, 16 * c)
                    weights = wide[:, row, :]
                dve.wait_ge(both_done, n + 1)
                wait_past(dve, hidlo_done, n - SLOTS + 1)
                nc.vector.tensor_tensor(hid[:, e % SLOTS, :], weights, both[e % SLOTS], ALU.mult).then_inc(hid_done, 1)

            def result(c):
                dve.wait_ge(fin_done, c + 1)
                wait_past(dve, stored, 16 * c)
                quads, x1 = (t.rearrange("p (q x y) -> p q x y", q=2, y=16)
                             for t in (sum_bank(c)[:, 0:2 * P], xs[:, bass.ds(2 * P * c, 2 * P)]))
                nc.vector.tensor_tensor(res[:, :].rearrange("p (x q y) -> p q x y", q=2, y=16), quads, x1, ALU.add).then_inc(res_done, 1)

            def chunk(c):
                for e in range(E):
                    n = E * c + e
                    if ce := before(c, e, WEIGH_LAG):
                        weigh(*ce)
                    dve.wait_ge(silu_done, n + 1)
                    dve.wait_ge(h2_done, n + 1)
                    wait_past(dve, hid_done, n - SLOTS + 1)
                    nc.vector.tensor_tensor(both[e % SLOTS], bank[2 + e % 2][:, :], gated[:, e % 2, :], ALU.mult).then_inc(both_done, 1)
                    if first_chunk(c) and e in (0, 2):
                        weights_out(CHUNKS // 4 + e)
                    if e == FIN_AT + 1 and not first_chunk(c):
                        result(c - 1)

            over_chunks(dve, chunk)
            for e in range(E - WEIGH_LAG, E):
                weigh(CHUNKS - 1, e)
            result(CHUNKS - 1)

        @block.gpsimd
        def _(pool):
            pool.wait_ge(zeroed, 1)
            for h in range(2):
                pool.dma_start(w_out_bd[h * C:(h + 1) * C, h * M:(h + 1) * M], w_out).then_inc(in_wout, 16)
            pool.dma_start(bw_rows[:, :], bin_w).then_inc(in_bw, 16)
            pool.wait_ge(rstd1_done, 1)
            nc.gpsimd.tensor_scalar(rstd1_1[:, :], rstd1[:, :], 1.0, None, ALU.add).then_inc(rstd1_1_done, 1)
            pool.wait_ge(rstd1_1_done, 1)
            for n in range(NBLK):
                nc.gpsimd.tensor_tensor(ct_cen[:, 4 * n:4 * n + 4, :, :], ct_cen[:, 4 * n:4 * n + 4, :, :],
                                        per_tile(rstd1_1[:, BT * n:BT * (n + 1)], C), ALU.mult).then_inc(base_done, 1)
            pool.wait_ge(in_gate, 16 * 3)
            nc.gpsimd.tensor_scalar(gate_raw[:, :], gate_raw[:, :], WSCALE, None, ALU.mult).then_inc(pool_own, 1)
            pool.wait_ge(pool_own, 1)
            nc.gpsimd.tensor_copy(gate_hi[:, :], gate_raw[:, :]).then_inc(pool_own, 1)
            pool.wait_ge(pool_own, 2)
            nc.gpsimd.tensor_tensor(gate_lo[:, :], gate_raw[:, :], gate_hi[:, :], ALU.subtract).then_inc(gate_set, 1)
            for n, (raw, hi, lo) in enumerate(weight_parts):
                pool.wait_ge(whi_done, n + 1)
                nc.gpsimd.tensor_tensor(lo, raw, hi, ALU.subtract).then_inc(wsplit, 1)

            for n in range(NBLK):
                pool.wait_ge(hi_done, n + 1)
                if n >= 2:
                    pool.wait_ge(xp_ps, n - 1)
                nc.gpsimd.tensor_tensor(parts[:, n % 2, :, 1, :], tok[:, n % 2, :, :], parts[:, n % 2, :, 0, :],
                                        ALU.subtract).then_inc(lo_done, 1)

            pool.wait_ge(mean1_done, 1)
            for n in range(NBLK):
                pool.wait_ge(tok_done, n + 1)
                nc.gpsimd.tensor_tensor(ct_cen[:, 4 * n:4 * n + 4, :, :], ct_cen[:, 4 * n:4 * n + 4, :, :],
                                        per_tile(mean1[:, BT * n:BT * (n + 1)], C), ALU.add).then_inc(x1t_done, 1)

            def low_part(c, e):
                n = E * c + e
                pool.wait_ge(hidhi_done, n + 1)
                wait_past(pool, down_done, n - PSLOTS + 1)
                nc.gpsimd.tensor_tensor(hid_lo[:, e % PSLOTS, :], hid[:, e % SLOTS, :], hid_hi[:, e % PSLOTS, :],
                                        ALU.subtract).then_inc(hidlo_done, 1)

            def sum_low_part(c):
                pool.wait_ge(ffnhi_done, c + 1)
                nc.gpsimd.tensor_tensor(ffn_lo[:, :], ffn[:, :], ffn_hi[:, :], ALU.subtract).then_inc(ffn_done, 1)

            def chunk(c):
                for e in range(E):
                    low_part(c, e)
                    if e == SUM_AT and not first_chunk(c):
                        sum_low_part(c - 1)

            over_chunks(pool, chunk)
            sum_low_part(CHUNKS - 1)


_INS = ["x", "L0_conv_w_in", "L0_conv_w_out", "L0_conv_bin_weights", "L0_ffn_gate_w", "L0_ffn_gate_b",
        "L0_ffn_w1", "L0_ffn_w2", "L0_ffn_w3"]


def kernel(**inputs):
    import concourse.bacc as bacc
    from concourse.bass_utils import run_bass_kernel_spmd

    nc = bacc.Bacc("TRN2", target_bir_lowering=False, num_devices=1)
    fwd, neg, inv = hartley_tables()
    tables = {"t_const": constant_tile(), "t_fwd": fwd, "t_neg": neg, "t_inv": inv, "t_bins": bin_table(), "t_sel": selector_table()}
    laid_out = {n: np.asarray(inputs[n]) for n in _INS}
    laid_out["L0_conv_w_in"] = laid_out["L0_conv_w_in"].T
    laid_out["L0_conv_bin_weights"] = laid_out["L0_conv_bin_weights"].reshape(M, AR).T
    for n in ("L0_ffn_w1", "L0_ffn_w2", "L0_ffn_w3"):
        laid_out[n] = laid_out[n].transpose(1, 0, 2)
    arrays, args = {}, []
    for name, a in list(laid_out.items()) + list(tables.items()):
        a = np.ascontiguousarray(a)
        arrays[f"in_{name}"] = a
        args.append(nc.dram_tensor(f"in_{name}", a.shape, mybir.dt.from_np(a.dtype), kind="ExternalInput").ap())
    args.append(nc.dram_tensor("out", (B, C, H, W), F32, kind="ExternalOutput").ap())
    build(nc, *args)
    r = run_bass_kernel_spmd(nc, [arrays], core_ids=[0])
    return r.results[0]["out"]
```
